# Optimizing a Trainium2 kernel written in Bass

```python
import numpy as np
import jax
import jax.numpy as jnp

def _softmax(x, axis=-1):
    return jax.nn.softmax(x, axis=axis)

def _gelu(x):
    return jax.nn.gelu(x, approximate=True)

def _silu(x):
    return jax.nn.silu(x)

def _sigmoid(x):
    return jax.nn.sigmoid(x)

def _layernorm(x, axis=-1, eps=1e-05):
    m = jnp.mean(x, axis=axis, keepdims=True)
    v = jnp.var(x, axis=axis, keepdims=True)
    return (x - m) / jnp.sqrt(v + eps)

def _scatter_add(tgt, idx, src, axis=0):
    return tgt.at[idx].add(src)

def _segment_sum(src, seg, n):
    return jax.ops.segment_sum(src, seg, n)
kernel_name = 'mk_hybrid_d1_jaxref_r8_02353d'

def setup_inputs(seed: int=0):
    np.random.seed(seed)
    _w = jnp.asarray

    def _L0_attn_a_setup():
        import jax, jax.numpy as jnp
        import numpy as np
        B, L, D_MODEL, D_STATE = (8, 512, 128, 64)
        key = jax.random.key(seed)
        k1, k2, k3, k4 = jax.random.split(key, 4)
        u = jax.random.normal(k1, (B, L, D_MODEL), dtype=jnp.float32)
        A_log = jnp.log(jnp.arange(1, D_STATE + 1, dtype=jnp.float32))
        D = jax.random.normal(k2, (D_MODEL,), dtype=jnp.float32)
        C_re = jax.random.normal(k3, (D_MODEL, D_STATE), dtype=jnp.float32)
        C_im = jax.random.normal(k4, (D_MODEL, D_STATE), dtype=jnp.float32)
        log_dt = jnp.log(jnp.full((D_MODEL,), 0.01, dtype=jnp.float32))
        return {'u': u, 'A_log': A_log, 'D': D, 'C_re': C_re, 'C_im': C_im, 'log_dt': log_dt}
    _L0_attn_a_in = _L0_attn_a_setup()

    def _L0_attn_b_setup():
        import math
        import jax, jax.numpy as jnp
        import numpy as np
        N_EMBD = 128
        N_HEAD = 16
        N_QUERY_SETS = 4
        B, T = (8, 128)
        key = jax.random.key(seed)
        kx, kw1, kw2 = jax.random.split(key, 3)
        C = N_EMBD
        x = jax.random.normal(kx, (B, T, C), dtype=jnp.float32)
        W_attn = jax.random.normal(kw1, ((N_QUERY_SETS + 2) * C, C), dtype=jnp.float32) * (1.0 / math.sqrt(C))
        W_proj = jax.random.normal(kw2, (C, N_QUERY_SETS * C), dtype=jnp.float32) * (1.0 / math.sqrt(N_QUERY_SETS * C))
        return {'x': x, 'W_attn': W_attn, 'W_proj': W_proj}
    _L0_attn_b_in = _L0_attn_b_setup()

    def _L0_ffn_setup():
        import jax, jax.numpy as jnp
        import numpy as np
        D_MODEL = 128
        NUM_EXPERTS = 8
        TOP_K = 2
        B, S = (4, 256)
        key = jax.random.key(seed)
        ks = jax.random.split(key, 7)
        scale_in = 1.0 / np.sqrt(D_MODEL)
        scale_hid = 1.0 / np.sqrt(2 * D_MODEL)
        return {'x': jax.random.normal(ks[0], (B, S, D_MODEL), dtype=jnp.float32), 'Wg': jax.random.normal(ks[1], (D_MODEL, NUM_EXPERTS), dtype=jnp.float32) * scale_in, 'bg': jnp.zeros((NUM_EXPERTS,), dtype=jnp.float32), 'W1': jax.random.normal(ks[2], (NUM_EXPERTS, D_MODEL, 2 * D_MODEL), dtype=jnp.float32) * scale_in, 'b1': jnp.zeros((NUM_EXPERTS, 2 * D_MODEL), dtype=jnp.float32), 'W2': jax.random.normal(ks[3], (NUM_EXPERTS, 2 * D_MODEL, D_MODEL), dtype=jnp.float32) * scale_hid, 'b2': jnp.zeros((NUM_EXPERTS, D_MODEL), dtype=jnp.float32)}
    _L0_ffn_in = _L0_ffn_setup()
    _d = {'L0_attn_a_u': _L0_attn_a_in['u'], 'L0_attn_a_A_log': _L0_attn_a_in['A_log'], 'L0_attn_a_D': _L0_attn_a_in['D'], 'L0_attn_a_C_re': _L0_attn_a_in['C_re'], 'L0_attn_a_C_im': _L0_attn_a_in['C_im'], 'L0_attn_a_log_dt': _L0_attn_a_in['log_dt'], 'L0_attn_b_W_attn': _L0_attn_b_in['W_attn'], 'L0_attn_b_W_proj': _L0_attn_b_in['W_proj'], 'L0_ffn_Wg': _L0_ffn_in['Wg'], 'L0_ffn_bg': _L0_ffn_in['bg'], 'L0_ffn_W1': _L0_ffn_in['W1'], 'L0_ffn_b1': _L0_ffn_in['b1'], 'L0_ffn_W2': _L0_ffn_in['W2'], 'L0_ffn_b2': _L0_ffn_in['b2']}
    _x0 = _d['L0_attn_a_u']
    _d['L0_attn_a_u'] = jax.random.normal(jax.random.fold_in(jax.random.key(seed), 1), (16, 256, 128), dtype=_x0.dtype)
    del _x0
    return _d

def reference(L0_attn_a_u, L0_attn_a_A_log, L0_attn_a_D, L0_attn_a_C_re, L0_attn_a_C_im, L0_attn_a_log_dt, L0_attn_b_W_attn, L0_attn_b_W_proj, L0_ffn_Wg, L0_ffn_bg, L0_ffn_W1, L0_ffn_b1, L0_ffn_W2, L0_ffn_b2):

    def _L0_attn_a_ref(u, A_log, D, C_re, C_im, log_dt):
        import jax, jax.numpy as jnp
        import numpy as np
        B, L, D_MODEL, D_STATE = (8, 512, 128, 64)
        L_ = u.shape[1]
        dt = jnp.exp(log_dt)
        A = -jnp.exp(A_log)
        t = jnp.arange(L_, dtype=u.dtype)
        at = dt[:, None, None] * A[None, None, :] * t[None, :, None]
        K = jnp.einsum('mn,mln->ml', C_re, jnp.exp(at))
        u_f = jnp.fft.rfft(u.transpose(0, 2, 1), n=2 * L_)
        k_f = jnp.fft.rfft(K, n=2 * L_)
        y = jnp.fft.irfft(u_f * k_f, n=2 * L_)[..., :L_]
        return y.transpose(0, 2, 1) + u * D

    def _L0_attn_b_ref(x, W_attn, W_proj):
        import math
        import jax, jax.numpy as jnp
        import numpy as np
        N_EMBD = 128
        N_HEAD = 16
        N_QUERY_SETS = 4
        B, T = (8, 128)
        Bz, Tz, C = x.shape
        hd = C // N_HEAD
        scale = 1.0 / math.sqrt(hd)
        qkv = x @ W_attn.T
        parts = jnp.split(qkv, N_QUERY_SETS + 2, axis=-1)
        k = parts[-2].reshape(Bz, Tz, N_HEAD, hd).transpose(0, 2, 1, 3)
        v = parts[-1].reshape(Bz, Tz, N_HEAD, hd).transpose(0, 2, 1, 3)
        causal = jnp.tril(jnp.ones((Tz, Tz), dtype=bool))
        outs = []
        for g in range(N_QUERY_SETS):
            q = parts[g].reshape(Bz, Tz, N_HEAD, hd).transpose(0, 2, 1, 3)
            att = jnp.einsum('bhqd,bhkd->bhqk', q, k) * scale
            att = jnp.where(causal, att, -jnp.inf)
            att = jax.nn.softmax(att, axis=-1)
            y = jnp.einsum('bhqk,bhkd->bhqd', att, v)
            outs.append(y.transpose(0, 2, 1, 3).reshape(Bz, Tz, C))
        combined = jnp.concatenate(outs, axis=-1)
        return combined @ W_proj.T

    def _L0_ffn_ref(x, Wg, bg, W1, b1, W2, b2):
        import jax, jax.numpy as jnp
        import numpy as np
        D_MODEL = 128
        NUM_EXPERTS = 8
        TOP_K = 2
        B, S = (4, 256)
        Bb, Ss, D = x.shape
        E = Wg.shape[1]
        xf = x.reshape(-1, D)
        logits = xf @ Wg + bg
        probs = jax.nn.softmax(logits, axis=-1)
        w, idx = jax.lax.top_k(probs, TOP_K)
        w = w / jnp.sum(w, axis=-1, keepdims=True)
        comb = jnp.sum(jax.nn.one_hot(idx, E, dtype=xf.dtype) * w[..., None], axis=1)
        h = jax.nn.relu(jnp.einsum('nd,edh->enh', xf, W1) + b1[:, None, :])
        y = jnp.einsum('enh,ehd->end', h, W2) + b2[:, None, :]
        out = jnp.einsum('end,ne->nd', y, comb)
        return out.reshape(Bb, Ss, D)
    x = L0_attn_a_u
    x = x + _L0_attn_a_ref(_layernorm(x, axis=-1), L0_attn_a_A_log, L0_attn_a_D, L0_attn_a_C_re, L0_attn_a_C_im, L0_attn_a_log_dt)
    x = x + _L0_ffn_ref(_layernorm(x, axis=-1), L0_ffn_Wg, L0_ffn_bg, L0_ffn_W1, L0_ffn_b1, L0_ffn_W2, L0_ffn_b2)
    x = x + _L0_attn_b_ref(_layernorm(x, axis=-1), L0_attn_b_W_attn, L0_attn_b_W_proj)
    x = x + _L0_ffn_ref(_layernorm(x, axis=-1), L0_ffn_Wg, L0_ffn_bg, L0_ffn_W1, L0_ffn_b1, L0_ffn_W2, L0_ffn_b2)
    return x

_drawn_inputs = setup_inputs


def setup_inputs(seed=0):
    import zlib

    import numpy as np

    out = dict(_drawn_inputs(seed))
    spreads = {'L0_attn_a_log_dt': (-4.605170249938965, 0.2),
     'L0_ffn_bg': (0.0, 0.8),
     'L0_ffn_b1': (0.0, 0.8),
     'L0_ffn_b2': (0.0, 0.8)}
    factors = {}
    for name, (base, spread) in spreads.items():
        noise = np.random.default_rng([zlib.crc32(name.encode()), seed]).standard_normal(out[name].shape)
        drawn = base * np.exp(spread * noise) if base else spread * noise
        out[name] = jnp.asarray(drawn.astype(out[name].dtype))
    for name, factor in factors.items():
        out[name] = (out[name] * factor).astype(out[name].dtype)
    return out
```

```python
import math
from contextlib import ExitStack

import numpy as np

import concourse.bass as bass
from concourse import mybir

F32 = mybir.dt.float32
F16 = mybir.dt.float16
U32 = mybir.dt.uint32
ALU = mybir.AluOpType
ACT = mybir.ActivationFunctionType
AX_X = mybir.AxisListType.X

P = 128
BATCH, SEQ, D = 16, 256, 128
HALVES = SEQ // P
TILES = BATCH * HALVES
STATES = 64
EXPERTS, HIDDEN = 8, 256
HBLK = HIDDEN // P
HEADS, SETS = 16, 4
HD = D // HEADS
EPS = 1e-5
FREQ = 2 * SEQ
BANK = 512

CONV_BATCHES = 4
CONV_CHUNKS = BATCH // CONV_BATCHES
FFN_TILES = 4
FFN_CHUNKS = TILES // FFN_TILES

QUADS, LANES = 4, 4
SLOT = 32
PARTS = 4
NSTACK = SETS * QUADS
SCALE = 1.0 / math.sqrt(HD)
PAIRS = SETS // 2
UNIT = 3 * 2 * P

RDEN_MIN, RDEN_MAX = 1e-15, 1e25
MASKED = -1e38


def dft_constants():
    n = np.arange(SEQ)
    f = np.arange(SEQ)
    ang = 2.0 * np.pi * np.outer(f, n) / FREQ
    cos, sin = np.cos(ang), -np.sin(ang)
    nyq = np.cos(np.pi * n)
    sin_packed = sin.copy()
    sin_packed[0] = nyq
    forward = np.concatenate([cos, sin_packed])
    cos_last = cos[:P].copy()
    cos_last[0] = nyq
    taps = np.concatenate([cos, sin, cos_last])
    weight = np.full((SEQ, 1), 2.0 / FREQ)
    weight[0] = 1.0 / FREQ
    inverse = np.concatenate([weight * cos, np.concatenate([nyq[None] / FREQ, (weight * sin)[1:]])])

    def by_sample(m):
        return np.ascontiguousarray(m.T.reshape(HALVES, P, m.shape[0]).transpose(1, 0, 2)).astype(np.float32)

    inv = np.ascontiguousarray(inverse.reshape(4, P, SEQ).transpose(1, 0, 2)).astype(np.float32)
    return by_sample(forward), by_sample(taps), inv


def shape_constants():
    forward, taps, inverse = dft_constants()
    k = np.arange(P)[:, None]
    q = np.arange(P)[None, :]
    keep = np.where(k <= q, 1.0, 0.0).astype(np.float32)
    return {
        "c_forward": forward,
        "c_taps": taps,
        "c_inverse": inverse,
        "c_ramp": np.tile(np.arange(SEQ, dtype=np.float32), (P, 1)),
        "c_eye": np.eye(P, dtype=np.float32),
        "c_keep": np.concatenate([keep, keep], axis=1),
        "c_masked": np.stack([np.where(np.arange(SEQ)[None, :] <= k + P * h, 0.0, MASKED) for h in range(HALVES)],
                             axis=1).astype(np.float32),
        "c_expert": np.tile(np.arange(EXPERTS, dtype=np.float32), (P, FFN_TILES, 1)),
    }


class Signal:

    def __init__(self, ctx, nc, name):
        self.sem, self.value = ctx.enter_context(nc.semaphore(name)), 0

    def add(self, n):
        self.value += n
        return (self, self.value)


class Stream:

    def __init__(self, name):
        self.name, self.items, self.seen = name, [], {}

    def wait(self, *events):
        for ev in events:
            if ev is None:
                continue
            signal, value = ev
            if self.seen.get(signal, 0) < value:
                self.seen[signal] = value
                self.items.append((signal.sem, value))

    def do(self, build, signal=None):
        self.items.append((build, signal.sem if signal else None, 1))
        return signal.add(1) if signal else None

    def dma(self, build, signal):
        self.items.append((build, signal.sem, 16))
        return signal.add(16)

    def branch(self, flag, body):
        def build(e):
            with e.If(e.value_load(flag[0:1, 0:1], min_val=0, max_val=1)):
                body(e)
        self.items.append((build, None, 1))

    def play(self, eng):
        for item in self.items:
            if len(item) == 2:
                eng.wait_ge(*item)
            else:
                ins = item[0](eng)
                if item[1] is not None:
                    ins.then_inc(item[1], item[2])


class Banks:

    def __init__(self, psum, numbers):
        self.views = [psum[:, n * BANK:(n + 1) * BANK] for n in numbers]
        self.free, self.at = [[] for _ in numbers], 0

    def take(self):
        i = self.at
        self.at = (i + 1) % len(self.views)
        before, self.free[i] = self.free[i], []
        return self.views[i], before, self.free[i]


def general_attention(ctx, nc, dr, psum, start, stream, normed, attended, wqkv, wproj, eye):
    own = ExitStack()

    def sb(name, shape, dt=F32):
        return own.enter_context(nc.sbuf_tensor(name, shape, dt))

    BH = BATCH * HEADS
    xt = sb("gen_xt", [P, SEQ])
    qk = sb("gen_qk", [P, SETS + 1, SEQ])
    vt = sb("gen_v", [P, HALVES, D])
    q_h, k_h = sb("gen_q_head", [HD, SETS, SEQ]), sb("gen_k_head", [HD, SEQ])
    v_h = sb("gen_v_head", [P, HALVES, HD])
    masked = sb("gen_masked", [P, HALVES, SEQ])
    raw = sb("gen_scores", [P, SETS, HALVES, SEQ])
    peak, shift = sb("gen_peak", [P, SETS * HALVES]), sb("gen_shift", [P, SETS * HALVES])
    weights = sb("gen_weights", [P, SETS * HALVES, SEQ])
    total, inv = sb("gen_total", [P, SETS * HALVES]), sb("gen_inverse", [P, SETS * HALVES])
    turned_w = sb("gen_turned", [P, SETS, 4 * P])
    o_h = sb("gen_out", [P, SETS * HALVES, HD])
    o_tok, o_rows = sb("gen_out_tokens", [P, SETS * D]), sb("gen_out_rows", [P, SETS * P])
    dq = nc.dram_tensor("gen_q", [BH, SETS, HD, SEQ], F32, kind="Internal").ap()
    dk = nc.dram_tensor("gen_k", [BH, HD, SEQ], F32, kind="Internal").ap()
    dv = nc.dram_tensor("gen_v_rows", [BH, SEQ, HD], F32, kind="Internal").ap()
    do = nc.dram_tensor("gen_o", [BH, SETS, SEQ, HD], F32, kind="Internal").ap()
    own.close()

    def sig(name):
        return Signal(ctx, nc, name)

    pe, act, dve, sync = (Stream(n) for n in ("tensor", "scalar", "vector", "sync"))
    p_g, a_g, v_g, s_g = sig("tensor_general"), sig("scalar_general"), sig("vector_general"), sig("landed_general")
    for q in (pe, act, dve, sync):
        q.wait(*start)
    mask_here = sync.dma(lambda e: e.dma_start(masked[:], dr["c_masked"]), s_g)

    wrote = None
    for b in range(BATCH):
        heads = slice(b * HEADS, (b + 1) * HEADS)
        pe.wait(wrote)
        for h in range(HALVES):
            done = pe.do(lambda e, h=h, b=b: e.transpose(psum[:, h * P:(h + 1) * P], normed[:, HALVES * b + h, :],
                                                         eye[:]), p_g)
        act.wait(done)
        done = act.do(lambda e: e.copy(xt[:], psum[:, 0:SEQ]), a_g)
        pe.wait(done)
        for g in range(SETS + 1):
            done = pe.do(lambda e, g=g: e.matmul(psum[:, (g + 1) * BANK:(g + 1) * BANK + SEQ],
                                                 wqkv[:, g * D:(g + 1) * D], xt[:], start=True, stop=True), p_g)
        for h in range(HALVES):
            done = pe.do(lambda e, h=h: e.matmul(psum[:, (6 + h) * BANK:(6 + h) * BANK + D],
                                                 xt[:, h * P:(h + 1) * P], wqkv[:, (SETS + 1) * D:(SETS + 2) * D],
                                                 start=True, stop=True), p_g)
        act.wait(done)
        for g in range(SETS + 1):
            act.do(lambda e, g=g: e.copy(qk[:, g, :], psum[:, (g + 1) * BANK:(g + 1) * BANK + SEQ]), a_g)
        for h in range(HALVES):
            done = act.do(lambda e, h=h: e.copy(vt[:, h, :], psum[:, (6 + h) * BANK:(6 + h) * BANK + D]), a_g)
        sync.wait(done)
        for g in range(SETS):
            sync.dma(lambda e, g=g, heads=heads: e.dma_start(dq[heads, g], qk[:, g, :]), s_g)
        sync.dma(lambda e, heads=heads: e.dma_start(dk[heads], qk[:, SETS, :]), s_g)
        for h in range(HALVES):
            wrote = sync.dma(lambda e, h=h, heads=heads: e.dma_start(
                dv[heads, h * P:(h + 1) * P, :].rearrange("n t d -> t n d"),
                vt[:, h, :].rearrange("t (n d) -> t n d", d=HD)), s_g)
    pe.wait(wrote)
    act.wait(wrote)
    dve.wait(wrote, mask_here)
    sync.wait(wrote)

    l_in, l_p, l_v, l_a, l_out = (sig(n) for n in ("loop_loads", "loop_tensor", "loop_vector", "loop_scalar",
                                                   "loop_stores"))
    IN, PEN, VN, AN, OUTN = 16 * (2 + HALVES), 3, 5, 2, 16 * SETS

    def loop_sync(e):
        e.sem_inc(l_out.sem, 1)
        with e.Fori(0, BH) as i:
            e.wait_ge(l_out.sem, i * OUTN + 1)
            e.dma_start(q_h[:], dq[bass.ds(i, 1)].rearrange("a g d t -> d (a g) t")).then_inc(l_in.sem, 16)
            e.dma_start(k_h[:], dk[bass.ds(i, 1)].rearrange("a d t -> d (a t)")).then_inc(l_in.sem, 16)
            for h in range(HALVES):
                e.dma_start(v_h[:, h, :], dv[bass.ds(i, 1), h * P:(h + 1) * P].rearrange("a t d -> t (a d)"))\
                 .then_inc(l_in.sem, 16)
            e.wait_ge(l_v.sem, i * VN + VN)
            for g in range(SETS):
                e.dma_start(do[bass.ds(i, 1), g].rearrange("a (h t) d -> t (a h) d", h=HALVES),
                            o_h[:, g * HALVES:(g + 1) * HALVES, :]).then_inc(l_out.sem, 16)

    def loop_pe(e):
        with e.Fori(0, BH) as i:
            e.wait_ge(l_in.sem, i * IN + IN)
            for g in range(SETS):
                for h in range(HALVES):
                    last = e.matmul(psum[:, g * BANK + h * SEQ:g * BANK + (h + 1) * SEQ], q_h[:, g, h * P:(h + 1) * P],
                                    k_h[:], start=True, stop=True)
            last.then_inc(l_p.sem, 1)
            e.wait_ge(l_v.sem, i * VN + 4)
            for g in range(SETS):
                for k in range(HALVES):
                    for h in range(HALVES):
                        at = (SETS + g) * BANK + (k * HALVES + h) * P
                        last = e.transpose(psum[:, at:at + P], weights[:, g * HALVES + h, k * P:(k + 1) * P], eye[:])
            last.then_inc(l_p.sem, 1)
            e.wait_ge(l_a.sem, i * AN + 2)
            for g in range(SETS):
                for h in range(HALVES):
                    for k in range(HALVES):
                        at = (k * HALVES + h) * P
                        last = e.matmul(psum[:, (g * HALVES + h) * HD:(g * HALVES + h + 1) * HD],
                                        turned_w[:, g, at:at + P], v_h[:, k, :], start=(k == 0), stop=(k == HALVES - 1))
            last.then_inc(l_p.sem, 1)

    def loop_dve(e):
        with e.Fori(0, BH) as i:
            e.wait_ge(l_p.sem, i * PEN + 1)
            for g in range(SETS):
                last = e.tensor_tensor(raw[:, g], psum[:, g * BANK:g * BANK + HALVES * SEQ].rearrange(
                    "p (h k) -> p h k", k=SEQ), masked[:], ALU.add)
            last.then_inc(l_v.sem, 1)
            e.wait_ge(l_v.sem, i * VN + 1)
            e.reduce_max(peak[:], raw[:].rearrange("p g h k -> p (g h) k"), AX_X).then_inc(l_v.sem, 1)
            e.wait_ge(l_v.sem, i * VN + 2)
            e.tensor_scalar(shift[:], peak[:], -SCALE, None, ALU.mult).then_inc(l_v.sem, 1)
            e.wait_ge(l_a.sem, i * AN + 1)
            e.reciprocal(inv[:], total[:]).then_inc(l_t.sem, 1)
            e.wait_ge(l_t.sem, i + 1)
            e.tensor_tensor(weights[:], weights[:], inv[:].rearrange("p (n a) -> p n a", a=1).to_broadcast(
                [P, SETS * HALVES, SEQ]), ALU.mult).then_inc(l_v.sem, 1)
            e.wait_ge(l_p.sem, i * PEN + 3)
            e.tensor_copy(o_h[:], psum[:, 0:SETS * HALVES * HD].rearrange("p (n d) -> p n d", d=HD))\
             .then_inc(l_v.sem, 1)

    l_t = sig("loop_inverse")

    def loop_act(e):
        with e.Fori(0, BH) as i:
            e.wait_ge(l_v.sem, i * VN + 3)
            for n in range(SETS * HALVES):
                last = e.activation(weights[:, n, :], raw[:, n // HALVES, n % HALVES, :], ACT.Exp, scale=SCALE,
                                    bias=shift[:, n:n + 1], accum_out=total[:, n:n + 1])
            last.then_inc(l_a.sem, 1)
            e.wait_ge(l_p.sem, i * PEN + 2)
            e.copy(turned_w[:].rearrange("p g n -> p (g n)"), psum[:, SETS * BANK:2 * SETS * BANK]).then_inc(l_a.sem, 1)

    tails = [Stream(n) for n in ("tensor", "scalar", "vector", "sync")]
    tpe, tact, tdve, tsync = tails
    stored = (l_out, BH * OUTN + 1)
    tsync.wait(stored)
    tpe.wait(stored)
    added = None
    for t in range(TILES):
        b, h = divmod(t, HALVES)
        tsync.wait(added)
        for n in range(HEADS):
            got = tsync.dma(lambda e, n=n, b=b, h=h: e.dma_start(
                o_tok[:].rearrange("p (g n d) -> p g n d", g=SETS, d=HD)[:, :, n, :],
                do[b * HEADS + n, :, h * P:(h + 1) * P, :].rearrange("g t d -> t g d")), s_g)
        tpe.wait(got)
        for g in range(SETS):
            done = tpe.do(lambda e, g=g: e.transpose(psum[:, g * P:(g + 1) * P], o_tok[:, g * D:(g + 1) * D], eye[:]), p_g)
        tact.wait(done)
        done = tact.do(lambda e: e.copy(o_rows[:], psum[:, 0:SETS * P]), a_g)
        tpe.wait(done)
        for g in range(SETS):
            done = tpe.do(lambda e, g=g: e.matmul(psum[:, BANK:BANK + D], o_rows[:, g * P:(g + 1) * P], wproj[:, g, :],
                                                  start=(g == 0), stop=(g == SETS - 1)), p_g)
        tdve.wait(done)
        added = tdve.do(lambda e, t=t: e.tensor_tensor(attended[:, t, :], psum[:, BANK:BANK + D], stream[:, t, :],
                                                       ALU.add), v_g)
    bodies = []
    for head, loop, tail in ((pe, loop_pe, tpe), (act, loop_act, tact), (dve, loop_dve, tdve),
                             (None, None, None), (sync, loop_sync, tsync)):
        def body(e, head=head, loop=loop, tail=tail):
            if head is not None:
                head.play(e)
                loop(e)
                tail.play(e)
            e.wait_ge(added[0].sem, added[1])
        bodies.append(body)
    return bodies


def build(nc, dr, out):
    with ExitStack() as ctx:
        def sb(name, shape, dt=F32):
            return ctx.enter_context(nc.sbuf_tensor(name, shape, dt))

        def sig(name):
            return Signal(ctx, nc, name)

        pe, act, dve, pool, sync = (Stream(n) for n in ("tensor", "scalar", "vector", "gpsimd", "sync"))
        psum = ctx.enter_context(nc.psum_tensor("psum", [P, 8 * BANK], F32))

        stream = sb("stream", [P, TILES, D])
        attended = sb("attended", [P, TILES, D])
        good = sb("good", [P, BATCH + 1])
        bad = sb("bad", [1, 1], mybir.dt.int32)
        normed = sb("normed", [P, TILES, D])
        stats = sb("stats", [P, TILES, 6])
        meanvar = sb("meanvar", [P, TILES, 2])
        rstd = sb("rstd", [P, TILES])
        vareps = sb("vareps", [P, TILES])
        minus_half = sb("minus_half", [P, TILES])
        eye = sb("eye", [P, P])
        ramp = sb("ramp", [P, SEQ])
        keep = sb("keep", [P, 2 * P])
        expert_no = sb("expert_no", [P, FFN_TILES, EXPERTS])
        wg = sb("wg", [P, EXPERTS])
        bg = sb("bg", [P, EXPERTS])
        w1 = sb("w1", [P, EXPERTS, HIDDEN])
        b1 = sb("b1", [P, EXPERTS * HBLK])
        w2 = sb("w2", [P, EXPERTS * HBLK, D])
        b2 = sb("b2", [EXPERTS, D])
        wqkv = sb("wqkv", [P, (SETS + 2) * D])
        wproj = sb("wproj", [P, SETS, D])

        s_const, s_small, s_dft, s_expw, s_attw = (sig(n) for n in (
            "landed_consts", "landed_small", "landed_dft", "landed_expert_weights", "landed_attn_weights"))
        s_x = [sig(f"landed_x{i}") for i in range(CONV_CHUNKS)]
        s_out = sig("landed_out")
        v_ln, g_ln = sig("vector_ln"), sig("gpsimd_ln")

        def load(dst, src, signal):
            return sync.dma(lambda e: e.dma_start(dst, src), signal)

        x_tiles = dr["L0_attn_a_u"].rearrange("b (h p) m -> p (b h) m", p=P)
        out_tiles = out.rearrange("b (h p) m -> p (b h) m", p=P)
        conv_ctx = ExitStack()

        def csb(name, shape, dt=F32):
            return conv_ctx.enter_context(nc.sbuf_tensor(name, shape, dt))

        a_log, c_re = csb("a_log", [P, STATES]), csb("c_re", [P, STATES])
        log_dt, skip_d = csb("log_dt", [P, 1]), csb("skip_d", [P, 1])
        forward = csb("forward", [P, HALVES, 4 * P])
        taps = csb("taps", [P, HALVES, 5 * P])
        inverse = csb("inverse", [P, 4, SEQ])
        load(a_log[:], dr["L0_attn_a_A_log"].rearrange("(a n) -> a n", a=1).to_broadcast([P, STATES]), s_small)
        load(log_dt[:], dr["L0_attn_a_log_dt"].rearrange("(p a) -> p a", a=1), s_small)
        load(c_re[:], dr["L0_attn_a_C_re"], s_small)
        load(skip_d[:], dr["L0_attn_a_D"].rearrange("(p a) -> p a", a=1), s_small)
        small_here = load(ramp[:], dr["c_ramp"], s_small)
        tiles_per = CONV_BATCHES * HALVES
        x_here = [load(stream[:, i * tiles_per:(i + 1) * tiles_per, :],
                       x_tiles[:, i * tiles_per:(i + 1) * tiles_per, :], s_x[i]) for i in range(CONV_CHUNKS)]
        load(eye[:], dr["c_eye"], s_dft)
        load(taps[:], dr["c_taps"], s_dft)
        load(forward[:], dr["c_forward"], s_dft)
        dft_here = load(inverse[:], dr["c_inverse"], s_dft)
        load(wg[:], dr["L0_ffn_Wg"], s_expw)
        load(bg[:], dr["L0_ffn_bg"].rearrange("(a n) -> a n", a=1).to_broadcast([P, EXPERTS]), s_expw)
        load(expert_no[:], dr["c_expert"], s_expw)
        load(b1[:], dr["b1_cols"], s_expw)
        load(b2[:], dr["L0_ffn_b2"], s_expw)
        load(w1[:], dr["L0_ffn_W1"].rearrange("e d h -> d e h"), s_expw)
        expw_here = load(w2[:], dr["L0_ffn_W2"].rearrange("e (k p) d -> p (e k) d", p=P), s_expw)
        load(keep[:], dr["c_keep"], s_attw)
        load(wqkv[:], dr["w_attn_cols"], s_attw)
        attw_here = load(wproj[:], dr["w_proj_rows"], s_attw)

        pow_ready = pool.do(lambda e: e.memset(minus_half[:], -0.5), g_ln)

        def layer_norm(x, t0, n, ready):
            dve.wait(*ready)
            for t in range(t0, t0 + n):
                stats_done = dve.do(lambda e, t=t: e.bn_stats(stats[:, t, :], x[:, t, :]), v_ln)
            dve.wait(stats_done)
            for t in range(t0, t0 + n):
                agg = dve.do(lambda e, t=t: e.bn_aggr(meanvar[:, t, :], stats[:, t, :]), v_ln)
            pool.wait(agg, pow_ready)
            eps_done = pool.do(lambda e: e.tensor_scalar(vareps[:, t0:t0 + n], meanvar[:, t0:t0 + n, 1], EPS, None,
                                                         ALU.add), g_ln)
            pool.wait(eps_done)
            rstd_done = pool.do(lambda e: e.tensor_tensor(rstd[:, t0:t0 + n], vareps[:, t0:t0 + n],
                                                          minus_half[:, t0:t0 + n], ALU.pow), g_ln)
            yield
            dve.wait(rstd_done)
            for t in range(t0, t0 + n):
                done = dve.do(lambda e, t=t: e.tensor_scalar(normed[:, t, :], x[:, t, :], meanvar[:, t, 0:1],
                                                             rstd[:, t:t + 1], ALU.subtract, ALU.mult), v_ln)
            yield done

        def last(gen):
            got = None
            for got in gen:
                pass
            return got

        a_k, v_k, p_k = sig("scalar_taps"), sig("vector_taps"), sig("tensor_taps")
        v_y, g_y, p_f, p_y = sig("vector_conv"), sig("gpsimd_conv"), sig("tensor_forward"), sig("tensor_inverse")
        CHAINS, ERING = 4, 8
        neg_a, dt, z = csb("neg_a", [P, STATES]), csb("dt", [P, 1]), csb("z", [P, STATES])
        decay = csb("decay", [P, ERING, SEQ])
        chain = csb("chain", [P, CHAINS, SEQ])
        ktap = csb("ktap", [P, HALVES, D])
        khat = csb("khat", [P, 5, D])

        act.wait(small_here)
        act.do(lambda e: e.activation(neg_a[:], a_log[:], ACT.Exp), a_k)
        exps_done = act.do(lambda e: e.activation(dt[:], log_dt[:], ACT.Exp), a_k)
        dve.wait(exps_done)
        z_done = dve.do(lambda e: e.tensor_scalar(z[:], neg_a[:], dt[:, 0:1], -1.0, ALU.mult, ALU.mult), v_k)
        act.wait(z_done)
        dve.wait(small_here)
        mac_done = []
        ln0 = layer_norm(stream, 0, tiles_per, [x_here[0]])
        for n in range(STATES):
            if n >= ERING:
                act.wait(mac_done[n - ERING])
            decayed = act.do(lambda e, n=n: e.activation(decay[:, n % ERING, :], ramp[:], ACT.Exp,
                                                         scale=z[:, n:n + 1]), a_k)
            dve.wait(decayed)
            c = n % CHAINS
            if n < CHAINS:
                mac_done.append(dve.do(lambda e, n=n, c=c: e.tensor_scalar(
                    chain[:, c, :], decay[:, n % ERING, :], c_re[:, n:n + 1], None, ALU.mult), v_k))
            else:
                dve.wait(mac_done[n - CHAINS])
                mac_done.append(dve.do(lambda e, n=n, c=c: e.scalar_tensor_tensor(
                    out=chain[:, c, :], in0=decay[:, n % ERING, :], scalar=c_re[:, n:n + 1],
                    in1=chain[:, c, :], op0=ALU.mult, op1=ALU.add), v_k))
        dve.wait(mac_done[-1])
        summed = dve.do(lambda e: e.tensor_tensor(chain[:, 0:2, :], chain[:, 0:2, :], chain[:, 2:4, :], ALU.add), v_k)
        dve.wait(summed)
        summed = dve.do(lambda e: e.tensor_tensor(chain[:, 0, :], chain[:, 0, :], chain[:, 1, :], ALU.add), v_k)
        dve.wait(summed)
        taps_done = dve.do(lambda e: e.tensor_tensor(chain[:, 0, 0:1], chain[:, 0, 0:1], skip_d[:], ALU.add), v_k)

        kb = Banks(psum, [6, 7])
        pe.wait(taps_done, dft_here)
        bank, before, free = kb.take()
        for h in range(HALVES):
            turned = pe.do(lambda e, h=h, bank=bank: e.transpose(bank[:, h * P:(h + 1) * P],
                                                                 chain[:, 0, h * P:(h + 1) * P], eye[:]), p_k)
        act.wait(turned)
        ktap_done = act.do(lambda e, bank=bank: e.copy(ktap[:], bank[:, 0:HALVES * P]), a_k)
        free.append(ktap_done)
        pe.wait(ktap_done)
        for lo, hi in ((0, 4), (4, 5)):
            bank, before, free = kb.take()
            pe.wait(*before)
            for i in range(lo, hi):
                for h in range(HALVES):
                    done = pe.do(lambda e, i=i, h=h, lo=lo, bank=bank: e.matmul(
                        bank[:, (i - lo) * P:(i - lo + 1) * P], taps[:, h, i * P:(i + 1) * P], ktap[:, h, :],
                        start=(h == 0), stop=(h == HALVES - 1)), p_k if h == HALVES - 1 else None)
            act.wait(done)
            khat_done = act.do(lambda e, lo=lo, hi=hi, bank=bank: e.copy(khat[:, lo:hi, :], bank[:, 0:(hi - lo) * P]),
                               a_k)
            free.append(khat_done)

        prod = csb("prod", [P, 2, 4, BANK])
        yhat = csb("yhat", [P, 2, 4, BANK])
        conv_done = []
        fb, ib = Banks(psum, [0, 1, 2, 3]), Banks(psum, [4, 5])
        yhat_read = [None, None]
        ln_ready = [last(ln0)]
        for ch in range(1, CONV_CHUNKS):
            ln_ready.append(last(layer_norm(stream, ch * tiles_per, tiles_per, [x_here[ch]])))
        fwd = {}

        def forward_chunk(ch):
            un = normed[:, ch * tiles_per:(ch + 1) * tiles_per, :].rearrange("p (b h) m -> p h b m", h=HALVES)
            pe.wait(ln_ready[ch])
            for i in (0, 2, 1, 3):
                bank, before, free = fb.take()
                pe.wait(*before)
                for h in range(HALVES):
                    done = pe.do(lambda e, i=i, h=h, bank=bank, un=un: e.matmul(
                        bank, forward[:, h, i * P:(i + 1) * P], un[:, h], start=(h == 0), stop=(h == HALVES - 1)),
                        p_f if h == HALVES - 1 else None)
                fwd[ch, i] = (bank, free, done)

        pe.wait(dft_here)
        forward_chunk(0)
        for ch in range(CONV_CHUNKS):
            s = ch % 2
            dve.wait(khat_done)
            y_done = []
            for f in range(2):
                (re, re_free, re_done), (im, im_free, im_done) = fwd[ch, f], fwd[ch, 2 + f]
                dve.wait(re_done, im_done)
                last_cos = 4 if f == 0 else 1
                for n, (src, free, k) in enumerate(((re, re_free, f), (im, im_free, 2 + f),
                                                    (re, re_free, 2 + f), (im, im_free, last_cos))):
                    dve.wait(yhat_read[s])
                    done = dve.do(lambda e, n=n, src=src, k=k, s=s: e.tensor_tensor(
                        prod[:, s, n, :].rearrange("p (b m) -> p b m", m=D), src.rearrange("p (b m) -> p b m", m=D),
                        khat[:, k:k + 1, :].to_broadcast([P, CONV_BATCHES, D]), ALU.mult), v_y)
                    if n >= 2:
                        free.append(done)
                pool.wait(done, yhat_read[s])
                eng_re = pool.do(lambda e, s=s, f=f: e.tensor_tensor(yhat[:, s, f, :], prod[:, s, 0, :], prod[:, s, 1, :],
                                                                     ALU.subtract), g_y)
                eng_im = pool.do(lambda e, s=s, f=f: e.tensor_tensor(yhat[:, s, 2 + f, :], prod[:, s, 2, :],
                                                                     prod[:, s, 3, :], ALU.add), g_y)
                if f == 0:
                    dve.wait(eng_im)
                y_done += [eng_re, eng_im]
            if ch + 1 < CONV_CHUNKS:
                forward_chunk(ch + 1)
            pe.wait(*y_done)
            for h in range(HALVES):
                bank, before, free = ib.take()
                pe.wait(*before)
                for i in range(4):
                    done = pe.do(lambda e, i=i, h=h, s=s, bank=bank: e.matmul(
                        bank, inverse[:, i, h * P:(h + 1) * P], yhat[:, s, i, :], start=(i == 0), stop=(i == 3)),
                        p_y if i == 3 else None)
                yhat_read[s] = done
                dve.wait(done)
                half = stream[:, ch * tiles_per:(ch + 1) * tiles_per, :].rearrange("p (b h) m -> p h b m", h=HALVES)[:, h]
                added = dve.do(lambda e, bank=bank, half=half: e.tensor_tensor(
                    half, bank.rearrange("p (b m) -> p b m", m=D), half, ALU.add), v_y)
                free.append(added)
            conv_done.append(added)
        conv_ctx.close()
        conv_over = [conv_done[-1], done]

        CH = FFN_TILES * P
        p_e, a_e, v_e = sig("tensor_experts"), sig("scalar_experts"), sig("vector_experts")

        def moe(tag, x, ready_of_tile, after_chunk, fence):
            own = ExitStack()

            def msb(name, shape, dt=F32):
                return own.enter_context(nc.sbuf_tensor(f"{name}_{tag}", shape, dt))

            xt = msb("xt", [P, 2, CH])
            logits = msb("logits", [P, 2, FFN_TILES, EXPERTS])
            top = msb("top", [P, 2, FFN_TILES, 8])
            top_at = msb("top_at", [P, 2, FFN_TILES, 8], U32)
            top_no = msb("top_no", [P, 2, FFN_TILES, 2])
            gap = msb("gap", [P, 2, FFN_TILES])
            wpair = msb("wpair", [P, 2, 2, FFN_TILES])
            pick = msb("pick", [P, 2, 2, FFN_TILES, EXPERTS])
            comb = msb("comb", [P, 2, FFN_TILES, EXPERTS])
            comb_t = msb("comb_t", [EXPERTS, 2, CH])
            hidden = msb("hidden", [P, 3, HBLK, CH])
            own.close()
            misc, hb, yb = Banks(psum, [6, 7]), Banks(psum, [0, 1, 2, 3]), Banks(psum, [4, 5])
            for bb in (misc, hb, yb):
                for f in bb.free:
                    f.extend(fence)
            for s_ in (act, dve, pool):
                s_.wait(*fence)
            xt_free, comb_free, combt_free, hid_free = [None] * 2, [None] * 2, [None] * 2, [None] * 3
            state = {}

            def prologue(ch):
                s, t0 = ch % 2, ch * FFN_TILES
                gen = layer_norm(x, t0, FFN_TILES, [ready_of_tile(t) for t in range(t0, t0 + FFN_TILES)])
                next(gen)
                yield
                normed_done = last(gen)
                yield
                bank, before, free = misc.take()
                pe.wait(normed_done, *before)
                for i in range(FFN_TILES):
                    done = pe.do(lambda e, i=i, bank=bank: e.transpose(bank[:, i * P:(i + 1) * P], normed[:, t0 + i, :],
                                                                       eye[:]), p_e if i == FFN_TILES - 1 else None)
                act.wait(done, xt_free[s])
                xt_done = act.do(lambda e, bank=bank: e.copy(xt[:, s, :], bank), a_e)
                free.append(xt_done)
                yield
                bank, before, free = misc.take()
                pe.wait(xt_done, *before)
                for i in range(FFN_TILES):
                    done = pe.do(lambda e, i=i, bank=bank: e.matmul(bank[:, i * EXPERTS:(i + 1) * EXPERTS],
                                                                    xt[:, s, i * P:(i + 1) * P], wg[:],
                                                                    start=True, stop=True),
                                 p_e if i == FFN_TILES - 1 else None)
                dve.wait(done)
                lg = logits[:, s]
                lg_done = dve.do(lambda e, bank=bank: e.tensor_tensor(
                    lg, bank[:, 0:FFN_TILES * EXPERTS].rearrange("p (t e) -> p t e", e=EXPERTS),
                    bg[:].rearrange("p (a e) -> p a e", a=1).to_broadcast([P, FFN_TILES, EXPERTS]), ALU.add), v_e)
                free.append(lg_done)
                dve.wait(lg_done)
                for i in range(FFN_TILES):
                    tops = dve.do(lambda e, i=i: e.max(top[:, s, i, :], logits[:, s, i, :]), v_e)
                dve.wait(tops)
                for i in range(FFN_TILES):
                    found = dve.do(lambda e, i=i: e.max_index(top_at[:, s, i, :], top[:, s, i, :], logits[:, s, i, :]),
                                   v_e)
                gap_done = dve.do(lambda e: e.tensor_tensor(gap[:, s, :], top[:, s, :, 1], top[:, s, :, 0],
                                                            ALU.subtract), v_e)
                act.wait(gap_done)
                ex_done = act.do(lambda e: e.activation(gap[:, s, :], gap[:, s, :], ACT.Exp), a_e)
                yield
                dve.wait(found)
                no_done = dve.do(lambda e: e.tensor_copy(top_no[:, s], top_at[:, s, :, 0:2]), v_e)
                dve.wait(ex_done)
                den = dve.do(lambda e: e.tensor_scalar(wpair[:, s, 1, :], gap[:, s, :], 1.0, None, ALU.add), v_e)
                dve.wait(den)
                w0 = dve.do(lambda e: e.reciprocal(wpair[:, s, 0, :], wpair[:, s, 1, :]), v_e)
                dve.wait(no_done, w0)
                w1_ = dve.do(lambda e: e.tensor_tensor(wpair[:, s, 1, :], wpair[:, s, 0, :], gap[:, s, :], ALU.mult), v_e)
                for k in range(2):
                    picked = dve.do(lambda e, k=k: e.tensor_tensor(
                        pick[:, s, k], expert_no[:], top_no[:, s, :, k:k + 1].to_broadcast([P, FFN_TILES, EXPERTS]),
                        ALU.is_equal), v_e)
                dve.wait(w1_, picked)
                for k in range(2):
                    scaled = dve.do(lambda e, k=k: e.tensor_tensor(
                        pick[:, s, k], pick[:, s, k],
                        wpair[:, s, k, :].rearrange("p (t a) -> p t a", a=1).to_broadcast([P, FFN_TILES, EXPERTS]),
                        ALU.mult), v_e)
                dve.wait(scaled, comb_free[s])
                comb_done = dve.do(lambda e: e.tensor_tensor(comb[:, s], pick[:, s, 0], pick[:, s, 1], ALU.add), v_e)
                yield
                bank, before, free = misc.take()
                pe.wait(comb_done, *before)
                for i in range(FFN_TILES):
                    done = pe.do(lambda e, i=i, bank=bank: e.transpose(bank[0:EXPERTS, i * P:(i + 1) * P],
                                                                       comb[:, s, i, :], eye[:]),
                                 p_e if i == FFN_TILES - 1 else None)
                act.wait(done, combt_free[s])
                ct_done = act.do(lambda e, bank=bank: e.copy(comb_t[:, s, :], bank[0:EXPERTS, :]), a_e)
                free.append(ct_done)
                yield
                bank, before, free = misc.take()
                pe.wait(ct_done, *before)
                for i in range(FFN_TILES):
                    done = pe.do(lambda e, i=i, bank=bank: e.matmul(bank[:, i * P:(i + 1) * P],
                                                                    comb_t[:, s, i * P:(i + 1) * P], b2[:],
                                                                    start=True, stop=True),
                                 p_e if i == FFN_TILES - 1 else None)
                combt_free[s] = done
                dve.wait(done, normed_done)
                base = dve.do(lambda e, bank=bank: e.tensor_tensor(
                    x[:, t0:t0 + FFN_TILES, :], bank.rearrange("p (t m) -> p t m", m=D),
                    x[:, t0:t0 + FFN_TILES, :], ALU.add), v_e)
                free.append(base)
                state[ch] = (xt_done, base)

            def up(ch, e_):
                s, r = ch % 2, (ch * EXPERTS + e_) % 3
                for k in range(HBLK):
                    bank, before, free = hb.take()
                    pe.wait(state[ch][0], *before)
                    done = pe.do(lambda e, k=k, bank=bank: e.matmul(bank, w1[:, e_, k * P:(k + 1) * P], xt[:, s, :],
                                                                    start=True, stop=True), p_e)
                    act.wait(done, hid_free[r])
                    relu = act.do(lambda e, k=k, bank=bank: e.activation(
                        hidden[:, r, k, :], bank, ACT.Relu, bias=b1[:, e_ * HBLK + k:e_ * HBLK + k + 1]), a_e)
                    free.append(relu)
                if e_ == EXPERTS - 1:
                    xt_free[s] = done
                return relu

            def down(ch, e_, relu):
                s, r, t0 = ch % 2, (ch * EXPERTS + e_) % 3, ch * FFN_TILES
                bank, before, free = yb.take()
                pe.wait(relu, *before)
                for i in range(FFN_TILES):
                    for k in range(HBLK):
                        done = pe.do(lambda e, i=i, k=k, bank=bank: e.matmul(
                            bank[:, i * P:(i + 1) * P], hidden[:, r, k, i * P:(i + 1) * P], w2[:, e_ * HBLK + k, :],
                            start=(k == 0), stop=(k == HBLK - 1)),
                            p_e if i == FFN_TILES - 1 and k == HBLK - 1 else None)
                hid_free[r] = done
                dve.wait(done, state[ch][1], state.get((ch, "acc")))
                for i in range(FFN_TILES):
                    acc = dve.do(lambda e, i=i, bank=bank: e.scalar_tensor_tensor(
                        out=x[:, t0 + i, :], in0=bank[:, i * P:(i + 1) * P], scalar=comb[:, s, i, e_:e_ + 1],
                        in1=x[:, t0 + i, :], op0=ALU.mult, op1=ALU.add), v_e)
                free.append(acc)
                state[ch, "acc"] = acc
                if e_ == EXPERTS - 1:
                    comb_free[s] = acc
                    after_chunk(ch, acc)

            pe.wait(expw_here)
            dve.wait(expw_here)
            act.wait(expw_here)
            for _ in prologue(0):
                pass
            pending = None
            for ch in range(FFN_CHUNKS):
                ahead = prologue(ch + 1) if ch + 1 < FFN_CHUNKS else iter(())
                for e_ in range(EXPERTS):
                    relu = up(ch, e_)
                    if pending:
                        down(*pending)
                    pending = (ch, e_, relu)
                    next(ahead, None)
                for _ in ahead:
                    pass
            down(*pending)
            return [acc_ for acc_ in (state[FFN_CHUNKS - 1, "acc"],)]

        ffn1_done = {}
        fence = moe("first", stream, lambda t: conv_done[t // tiles_per], lambda ch, acc: ffn1_done.__setitem__(ch, acc), conv_over)

        scratch = nc.dram_tensor("qk_parts", [2, 2, (SETS + 1) * D, SEQ], F16, kind="Internal").ap()
        att = ExitStack()

        def asb(name, shape, dt=F32):
            return att.enter_context(nc.sbuf_tensor(name, shape, dt))

        at_x = asb("at_x", [P, 2, SEQ])
        parts = asb("parts", [P, 2, 2, SETS + 1, SEQ], F16)
        qstack = asb("qstack", [P, 2, NSTACK, SEQ], F16)
        kstack = asb("kstack", [P, 2, HEADS, SEQ], F16)
        vstack = asb("vstack", [P, 2, HALVES, HEADS, SLOT])
        prob = asb("prob", [P, 3, LANES, UNIT])
        o_sb = asb("o_sb", [P, 2, BANK])
        o_tok = asb("o_tok", [P, 2, HALVES, SETS, D])
        rden = asb("rden", [P, BATCH, QUADS * PAIRS, 2 * 2 * LANES])
        in_range = asb("in_range", [P, QUADS * PAIRS * 2 * 2 * LANES])
        o_rows = asb("o_rows", [P, 2, BANK])
        p_a, a_a, v_a, g_a = sig("tensor_attn"), sig("scalar_attn"), sig("vector_attn"), sig("gpsimd_attn")
        s_parts = [sig(f"landed_parts{i}") for i in range(2)]
        s_stack = [sig(f"landed_stack{i}") for i in range(2)]

        misc, ob = Banks(psum, [6, 7]), Banks(psum, [4, 5])
        for bb in (misc, ob):
            for f in bb.free:
                f.extend(fence)
        score_banks = [psum[:, 2 * i * BANK:2 * i * BANK + UNIT] for i in range(2)]
        score_free = [list(fence), list(fence)]
        pool.wait(*conv_over, *fence)
        pool.do(lambda e: e.memset(kstack[:], 0.0), g_a)
        pool.do(lambda e: e.memset(vstack[:], 0.0), g_a)
        zeroed = (g_a, g_a.value)
        pool.wait(zeroed)
        zeroed = pool.do(lambda e: e.memset(vstack[:, :, :, :, HD:HD + 1], 1.0), g_a)
        for q_ in (pe, act, dve):
            q_.wait(*fence, attw_here)
        slot_free = {"x": [None] * 2, "parts": [None] * 2, "stack": [None] * 2, "v": [None] * 2,
                     "scratch": [None] * 2, "otok": [None] * 2}
        ready = {}

        def attn_prologue(b):
            s = b % 2
            gen = layer_norm(stream, HALVES * b, HALVES, [ffn1_done[HALVES * b // FFN_TILES]])
            next(gen)
            yield
            normed_done = last(gen)
            yield
            bank, before, free = misc.take()
            pe.wait(normed_done, *before)
            for h in range(HALVES):
                done = pe.do(lambda e, h=h, bank=bank: e.transpose(bank[:, h * P:(h + 1) * P],
                                                                   normed[:, HALVES * b + h, :], eye[:]),
                             p_a if h == HALVES - 1 else None)
            act.wait(done, slot_free["x"][s])
            x_done = act.do(lambda e, bank=bank: e.copy(at_x[:, s, :], bank[:, 0:SEQ]), a_a)
            free.append(x_done)
            yield
            for g0 in range(0, SETS + 1, 2):
                n = min(2, SETS + 1 - g0)
                bank, before, free = misc.take()
                pe.wait(x_done, *before)
                for g in range(g0, g0 + n):
                    done = pe.do(lambda e, g=g, g0=g0, bank=bank: e.matmul(
                        bank[:, (g - g0) * SEQ:(g - g0 + 1) * SEQ], wqkv[:, g * D:(g + 1) * D], at_x[:, s, :],
                        start=True, stop=True), p_a if g == g0 + n - 1 else None)
                act.wait(done, slot_free["parts"][s])
                src = bank[:, 0:n * SEQ].rearrange("p (g t) -> p g t", t=SEQ)
                hi = act.do(lambda e, g0=g0, n=n, src=src: e.copy(parts[:, s, 0, g0:g0 + n, :], src), a_a)
                dve.wait(hi)
                lo = dve.do(lambda e, g0=g0, n=n, src=src: e.tensor_tensor(
                    parts[:, s, 1, g0:g0 + n, :], src, parts[:, s, 0, g0:g0 + n, :], ALU.subtract), v_a)
                free.append(lo)
                yield
            sync.wait(lo, hi, slot_free["scratch"][s])
            wrote = sync.dma(lambda e: e.dma_start(scratch[s].rearrange("c (g r) t -> r c g t", r=P),
                                                   parts[:, s]), s_parts[s])
            slot_free["parts"][s] = wrote
            sync.wait(wrote, zeroed, slot_free["stack"][s])
            rows = scratch[s].rearrange("c (n l d) t -> c l d n t", l=LANES, d=HD)
            for lane in range(LANES):
                for part in range(PARTS):
                    at = SLOT * lane + HD * part
                    qsrc = rows[part // 2, lane, :, 0:NSTACK, :]
                    ksrc = rows[part % 2, lane, :, NSTACK:NSTACK + QUADS, :]
                    kdst = kstack[at:at + HD, s].rearrange("d (c l) t -> d c l t", l=LANES)[:, :, lane, :]
                    sync.dma(lambda e, at=at, qsrc=qsrc: e.dma_start(qstack[at:at + HD, s], qsrc), s_stack[s])
                    stacked = sync.dma(lambda e, kdst=kdst, ksrc=ksrc: e.dma_start(kdst, ksrc), s_stack[s])
            slot_free["scratch"][s] = stacked
            yield
            bank, before, free = misc.take()
            pe.wait(*before)
            for h in range(HALVES):
                done = pe.do(lambda e, h=h, bank=bank: e.matmul(bank[:, h * P:(h + 1) * P],
                                                                at_x[:, s, h * P:(h + 1) * P],
                                                                wqkv[:, (SETS + 1) * D:(SETS + 2) * D],
                                                                start=True, stop=True),
                             p_a if h == HALVES - 1 else None)
            slot_free["x"][s] = done
            act.wait(done, zeroed, slot_free["v"][s])
            v_done = act.do(lambda e, bank=bank: e.copy(
                vstack[:, s, :, :, 0:HD].rearrange("p h n d -> p (h n) d"),
                bank[:, 0:HALVES * D].rearrange("p (n d) -> p n d", d=HD)), a_a)
            free.append(v_done)
            ready[b] = (stacked, v_done)

        units = [0]
        probs_free = [None] * 3

        def scores(b, grp, lane):
            c, pair = divmod(grp, PAIRS)
            s, u, pb = b % 2, units[0] % 2, (b * QUADS * PAIRS + grp) % 3
            units[0] += 1
            qs = qstack[:, s].rearrange("p (g c) t -> p c g t", c=QUADS)[:, c, 2 * pair:2 * pair + 2, :]
            sbk = score_banks[u]
            pe.wait(ready[b][0], *score_free[u])
            pe.do(lambda e: e.matmul(sbk[:, 0:2 * SEQ], kstack[:, s, c * LANES + lane, 0:P],
                                     qs.rearrange("p g (h q) -> p h g q", q=P), start=True, stop=True))
            done = pe.do(lambda e: e.matmul(sbk[:, 2 * SEQ:UNIT], kstack[:, s, c * LANES + lane, P:SEQ],
                                            qs[:, :, P:SEQ], start=True, stop=True), p_a)
            if grp == QUADS * PAIRS - 1 and lane == LANES - 1:
                slot_free["stack"][s] = done
            act.wait(done, probs_free[pb])
            ex = act.do(lambda e: e.activation(prob[:, pb, lane, :], sbk, ACT.Exp, scale=SCALE), a_a)
            score_free[u] = [ex]
            eng, sg = (pool, g_a) if lane == LANES - 1 else (dve, v_a)
            diag = prob[:, pb, lane, :].rearrange("p (n q) -> p n q", q=2 * P)[:, 0:3:2, :]
            eng.wait(ex)
            return eng.do(lambda e: e.tensor_tensor(
                diag, diag, keep[:].rearrange("p (a q) -> p a q", a=1).to_broadcast([P, 2, 2 * P]), ALU.mult), sg), ex

        def weighted(b, grp, half, masked, bank, before):
            c, _ = divmod(grp, PAIRS)
            s, pb = b % 2, (b * QUADS * PAIRS + grp) % 3
            if half == 0:
                pe.wait(*before, ready[b][1])
            for m, ex in masked:
                pe.wait(m)
            for lane in range(LANES):
                o = bank[SLOT * lane:SLOT * (lane + 1)]
                if half == 0:
                    done = pe.do(lambda e, lane=lane, o=o: e.matmul(
                        o, vstack[:, s, 0, c * LANES + lane, :], prob[:, pb, lane, 0:2 * SEQ],
                        start=True, stop=False))
                else:
                    done = pe.do(lambda e, lane=lane, o=o: e.matmul(
                        o[:, SEQ:2 * SEQ], vstack[:, s, 1, c * LANES + lane, :], prob[:, pb, lane, 2 * SEQ:UNIT],
                        start=False, stop=True), p_a if lane == LANES - 1 else None)
            if half == 1:
                probs_free[pb] = done
                if grp == QUADS * PAIRS - 1:
                    slot_free["v"][s] = done
            return done

        o_free = [None] * 2

        def turn(b, grp, bank, free, done):
            s, r = b % 2, grp % 2
            c, pair = divmod(grp, PAIRS)
            act.wait(done, o_free[r])
            copied = act.do(lambda e: e.copy(o_sb[:, r, :], bank), a_a)
            free.append(copied)
            tb, before, tfree = misc.take()
            pe.wait(copied, *before)
            for n in range(4):
                done = pe.do(lambda e, n=n: e.transpose(tb[:, n * P:(n + 1) * P], o_sb[:, r, n * P:(n + 1) * P], eye[:]),
                             p_a if n == 3 else None)
            o_free[r] = done
            heads = tb.rearrange("p (n r) -> p n r", r=SLOT)
            rd = rden[:, b, grp, :].rearrange("p (n a) -> p n a", a=1)
            dve.wait(done)
            rec = dve.do(lambda e: e.reciprocal(rd, heads[:, :, HD:HD + 1]), v_a)
            dve.wait(rec, slot_free["otok"][s] if grp == 0 else None)
            nrm = dve.do(lambda e: e.tensor_tensor(
                o_tok[:, s, :, 2 * pair:2 * pair + 2, c * SLOT:(c + 1) * SLOT].rearrange("p h k (j d) -> p h k j d", d=HD),
                heads[:, :, 0:HD].rearrange("p (h k j) d -> p h k j d", h=HALVES, k=2),
                rd.rearrange("p (h k j) a -> p h k j a", h=HALVES, k=2).to_broadcast([P, HALVES, 2, LANES, HD]),
                ALU.mult), v_a)
            tfree.append(nrm)
            return nrm

        attn_done = {}
        rows_free = [None] * 2
        counted = [None]

        def attn_epilogue(b, nrm):
            s = b % 2
            rd = rden[:, b].rearrange("p g n -> p (g n)")
            dve.wait(nrm)
            low = dve.do(lambda e: e.tensor_scalar(in_range[:], rd, RDEN_MIN, None, ALU.is_ge), v_a)
            dve.wait(low)
            counted[0] = dve.do(lambda e: e.scalar_tensor_tensor(
                out=in_range[:], in0=rd, scalar=RDEN_MAX, in1=in_range[:], op0=ALU.is_le, op1=ALU.mult,
                accum_out=good[:, b:b + 1]), v_a)
            for h in range(HALVES):
                bank, before, free = misc.take()
                pe.wait(nrm, *before)
                for g in range(SETS):
                    done = pe.do(lambda e, g=g, h=h, bank=bank: e.transpose(
                        bank[:, g * P:(g + 1) * P], o_tok[:, s, h, g, :], eye[:]), p_a if g == SETS - 1 else None)
                act.wait(done, rows_free[h])
                copied = act.do(lambda e, h=h, bank=bank: e.copy(o_rows[:, h, :], bank), a_a)
                free.append(copied)
                if h == HALVES - 1:
                    slot_free["otok"][s] = done
                yield
                bank, before, free = misc.take()
                pe.wait(copied, *before)
                for g in range(SETS):
                    done = pe.do(lambda e, g=g, h=h, bank=bank: e.matmul(
                        bank[:, 0:D], o_rows[:, h, g * P:(g + 1) * P], wproj[:, g, :], start=(g == 0),
                        stop=(g == SETS - 1)), p_a if g == SETS - 1 else None)
                rows_free[h] = done
                t = HALVES * b + h
                dve.wait(done)
                added = dve.do(lambda e, t=t, bank=bank: e.tensor_tensor(attended[:, t, :], bank[:, 0:D],
                                                                         stream[:, t, :], ALU.add), v_a)
                free.append(added)
                attn_done[t] = added
                yield

        for _ in attn_prologue(0):
            pass
        NG = QUADS * PAIRS
        steps = [(b, g) for b in range(BATCH) for g in range(NG)]
        prev, ahead, behind, prev_turn = None, iter(()), iter(()), None
        for b, g in steps:
            if g == 0:
                for _ in ahead:
                    pass
                ahead = attn_prologue(b + 1) if b + 1 < BATCH else iter(())
            masked = [scores(b, g, 0), scores(b, g, 1)]
            if prev:
                (pb_, pg_, pm_) = prev
                bank, before, free = ob.take()
                weighted(pb_, pg_, 0, pm_, bank, before)
            masked += [scores(b, g, 2), scores(b, g, 3)]
            if prev:
                done = weighted(pb_, pg_, 1, pm_, bank, before)
                if prev_turn:
                    nrm = turn(*prev_turn)
                    if prev_turn[1] == NG - 1:
                        for _ in behind:
                            pass
                        behind = attn_epilogue(prev_turn[0], nrm)
                prev_turn = (pb_, pg_, bank, free, done)
            next(ahead, None)
            next(behind, None)
            next(ahead, None)
            prev = (b, g, masked)
        for _ in behind:
            pass
        nrm = turn(*prev_turn)
        bank, before, free = ob.take()
        weighted(prev[0], prev[1], 0, prev[2], bank, before)
        done = weighted(prev[0], prev[1], 1, prev[2], bank, before)
        nrm = turn(prev[0], prev[1], bank, free, done)
        for _ in attn_epilogue(BATCH - 1, nrm):
            pass
        dve.wait(counted[0])
        counted[0] = dve.do(lambda e: e.reduce_sum(good[:, BATCH:BATCH + 1], good[:, 0:BATCH], AX_X), v_a)
        bank, before, free = misc.take()
        pe.wait(counted[0], *before)
        turned = pe.do(lambda e: e.transpose(bank[0:1, 0:P], good[:, BATCH:BATCH + 1], eye[:]), p_a)
        dve.wait(turned)
        counted[0] = dve.do(lambda e: e.reduce_sum(good[0:1, 0:1], bank[0:1, 0:P], AX_X), v_a)
        dve.wait(counted[0])
        bad_known = dve.do(lambda e: e.tensor_scalar(bad[:], good[0:1, 0:1], float(BATCH * SEQ * HEADS * SETS) - 0.5,
                                                     None, ALU.is_lt), v_a)
        att.close()
        main_over = [bad_known, attn_done[TILES - 1], (p_a, p_a.value), (a_a, a_a.value), (g_a, g_a.value)]
        for q_ in (pe, act, dve, pool, sync):
            q_.wait(*main_over)
        general = general_attention(ctx, nc, dr, psum, main_over, stream, normed, attended, wqkv, wproj, eye)
        for q_, g_ in zip((pe, act, dve, pool, sync), general):
            q_.branch(bad, g_)

        def store(ch, acc):
            sync.wait(acc)
            t0 = ch * FFN_TILES
            sync.dma(lambda e: e.dma_start(out_tiles[:, t0:t0 + FFN_TILES, :], attended[:, t0:t0 + FFN_TILES, :]), s_out)

        moe("second", attended, lambda t: None, store, [])
        sync.wait((s_out, s_out.value))

        block = ctx.enter_context(nc.Block())
        block.sync(lambda e: sync.play(e))
        block.gpsimd(lambda e: pool.play(e))
        block.scalar(lambda e: act.play(e))
        block.vector(lambda e: dve.play(e))
        block.tensor(lambda e: pe.play(e))


OUT_SHAPE = (BATCH, SEQ, D)


def kernel(**inputs):
    import concourse.bacc as bacc
    from concourse.bass_utils import run_bass_kernel_spmd

    arrays = {k: np.ascontiguousarray(v) for k, v in inputs.items()
              if k not in ("L0_attn_b_W_attn", "L0_attn_b_W_proj", "L0_ffn_b1", "L0_attn_a_C_im")}
    arrays["w_attn_cols"] = np.ascontiguousarray(np.asarray(inputs["L0_attn_b_W_attn"]).T)
    arrays["w_proj_rows"] = np.ascontiguousarray(
        np.asarray(inputs["L0_attn_b_W_proj"]).T.reshape(SETS, P, D).transpose(1, 0, 2))
    arrays["b1_cols"] = np.ascontiguousarray(np.asarray(inputs["L0_ffn_b1"]).reshape(EXPERTS * HBLK, P).T)
    arrays.update(shape_constants())
    nc = bacc.Bacc("TRN2", target_bir_lowering=False, num_devices=1)
    dr = {k: nc.dram_tensor(k, a.shape, mybir.dt.from_np(a.dtype), kind="ExternalInput").ap()
          for k, a in arrays.items()}
    out = nc.dram_tensor("out", OUT_SHAPE, F32, kind="ExternalOutput").ap()
    build(nc, dr, out)
    r = run_bass_kernel_spmd(nc, [arrays], core_ids=[0])
    return r.results[0]["out"]
```

```python
import math
from contextlib import ExitStack

import numpy as np

import concourse.bass as bass
from concourse import mybir

F32 = mybir.dt.float32
F16 = mybir.dt.float16
U32 = mybir.dt.uint32
ALU = mybir.AluOpType
ACT = mybir.ActivationFunctionType
AX_X = mybir.AxisListType.X

P = 128
BATCH, SEQ, D = 16, 256, 128
HALVES = SEQ // P
TILES = BATCH * HALVES
STATES = 64
EXPERTS, HIDDEN = 8, 256
HBLK = HIDDEN // P
HEADS, SETS = 16, 4
HD = D // HEADS
EPS = 1e-5
FREQ = 2 * SEQ
BANK = 512

CONV_BATCHES = 4
CONV_CHUNKS = BATCH // CONV_BATCHES
FFN_TILES = 4
FFN_CHUNKS = TILES // FFN_TILES

QUADS, LANES = 4, 4
SLOT = 32
SCALE = 1.0 / math.sqrt(HD)
PAIRS = SETS // 2
UNIT = 3 * 2 * P

RDEN_MIN, RDEN_MAX = 1e-15, 1e25
MASKED = -1e38


def dft_constants():
    n = np.arange(SEQ)
    f = np.arange(SEQ)
    ang = 2.0 * np.pi * np.outer(f, n) / FREQ
    cos, sin = np.cos(ang), -np.sin(ang)
    nyq = np.cos(np.pi * n)
    sin_packed = sin.copy()
    sin_packed[0] = nyq
    forward = np.concatenate([cos, sin_packed])
    cos_last = cos[:P].copy()
    cos_last[0] = nyq
    taps = np.concatenate([cos, sin, cos_last])
    weight = np.full((SEQ, 1), 2.0 / FREQ)
    weight[0] = 1.0 / FREQ
    inverse = np.concatenate([weight * cos, np.concatenate([nyq[None] / FREQ, (weight * sin)[1:]])])

    def by_sample(m):
        return np.ascontiguousarray(m.T.reshape(HALVES, P, m.shape[0]).transpose(1, 0, 2)).astype(np.float32)

    inv = np.ascontiguousarray(inverse.reshape(4, P, SEQ).transpose(1, 0, 2)).astype(np.float32)
    return by_sample(forward), by_sample(taps), inv


def shape_constants():
    forward, taps, inverse = dft_constants()
    k = np.arange(P)[:, None]
    q = np.arange(P)[None, :]
    keep = np.where(k <= q, 1.0, 0.0).astype(np.float32)
    return {
        "c_forward": forward,
        "c_taps": taps,
        "c_inverse": inverse,
        "c_ramp": np.tile(np.arange(SEQ, dtype=np.float32), (P, 1)),
        "c_eye": np.eye(P, dtype=np.float32),
        "c_keep": np.concatenate([keep, keep], axis=1),
        "c_masked": np.stack([np.where(np.arange(SEQ)[None, :] <= k + P * h, 0.0, MASKED) for h in range(HALVES)],
                             axis=1).astype(np.float32),
        "c_lanes": (np.arange(P)[:, None] // HD % LANES == np.arange(LANES)[None, :]).astype(np.float32),
        "c_expert": np.tile(np.arange(EXPERTS, dtype=np.float32), (P, FFN_TILES, 1)),
    }


class Signal:

    def __init__(self, ctx, nc, name):
        self.sem, self.value = ctx.enter_context(nc.semaphore(name)), 0

    def add(self, n):
        self.value += n
        return (self, self.value)


class Stream:

    def __init__(self, name):
        self.name, self.items, self.seen = name, [], {}

    def wait(self, *events):
        for ev in events:
            if ev is None:
                continue
            signal, value = ev
            if self.seen.get(signal, 0) < value:
                self.seen[signal] = value
                self.items.append((signal.sem, value))

    def do(self, build, signal=None):
        self.items.append((build, signal.sem if signal else None, 1))
        return signal.add(1) if signal else None

    def dma(self, build, signal):
        self.items.append((build, signal.sem, 16))
        return signal.add(16)

    def branch(self, flag, body):
        def build(e):
            with e.If(e.value_load(flag[0:1, 0:1], min_val=0, max_val=1)):
                body(e)
        self.items.append((build, None, 1))

    def play(self, eng):
        for item in self.items:
            if len(item) == 2:
                eng.wait_ge(*item)
            else:
                ins = item[0](eng)
                if item[1] is not None:
                    ins.then_inc(item[1], item[2])


class Banks:

    def __init__(self, psum, numbers):
        self.views = [psum[:, n * BANK:(n + 1) * BANK] for n in numbers]
        self.free, self.at = [[] for _ in numbers], 0

    def take(self):
        i = self.at
        self.at = (i + 1) % len(self.views)
        before, self.free[i] = self.free[i], []
        return self.views[i], before, self.free[i]


def general_attention(ctx, nc, dr, psum, start, stream, normed, attended, wqkv, wproj, eye):
    own = ExitStack()

    def sb(name, shape, dt=F32):
        return own.enter_context(nc.sbuf_tensor(name, shape, dt))

    BH = BATCH * HEADS
    xt = sb("gen_xt", [P, SEQ])
    qk = sb("gen_qk", [P, SETS + 1, SEQ])
    vt = sb("gen_v", [P, HALVES, D])
    q_h, k_h = sb("gen_q_head", [HD, SETS, SEQ]), sb("gen_k_head", [HD, SEQ])
    v_h = sb("gen_v_head", [P, HALVES, HD])
    masked = sb("gen_masked", [P, HALVES, SEQ])
    raw = sb("gen_scores", [P, SETS, HALVES, SEQ])
    peak, shift = sb("gen_peak", [P, SETS * HALVES]), sb("gen_shift", [P, SETS * HALVES])
    weights = sb("gen_weights", [P, SETS * HALVES, SEQ])
    total, inv = sb("gen_total", [P, SETS * HALVES]), sb("gen_inverse", [P, SETS * HALVES])
    turned_w = sb("gen_turned", [P, SETS, 4 * P])
    o_h = sb("gen_out", [P, SETS * HALVES, HD])
    o_tok, o_rows = sb("gen_out_tokens", [P, SETS * D]), sb("gen_out_rows", [P, SETS * P])
    dq = nc.dram_tensor("gen_q", [BH, SETS, HD, SEQ], F32, kind="Internal").ap()
    dk = nc.dram_tensor("gen_k", [BH, HD, SEQ], F32, kind="Internal").ap()
    dv = nc.dram_tensor("gen_v_rows", [BH, SEQ, HD], F32, kind="Internal").ap()
    do = nc.dram_tensor("gen_o", [BH, SETS, SEQ, HD], F32, kind="Internal").ap()
    own.close()

    def sig(name):
        return Signal(ctx, nc, name)

    pe, act, dve, sync = (Stream(n) for n in ("tensor", "scalar", "vector", "sync"))
    p_g, a_g, v_g, s_g = sig("tensor_general"), sig("scalar_general"), sig("vector_general"), sig("landed_general")
    for q in (pe, act, dve, sync):
        q.wait(*start)
    mask_here = sync.dma(lambda e: e.dma_start(masked[:], dr["c_masked"]), s_g)

    wrote = None
    for b in range(BATCH):
        heads = slice(b * HEADS, (b + 1) * HEADS)
        pe.wait(wrote)
        for h in range(HALVES):
            done = pe.do(lambda e, h=h, b=b: e.transpose(psum[:, h * P:(h + 1) * P], normed[:, HALVES * b + h, :],
                                                         eye[:]), p_g)
        act.wait(done)
        done = act.do(lambda e: e.copy(xt[:], psum[:, 0:SEQ]), a_g)
        pe.wait(done)
        for g in range(SETS + 1):
            done = pe.do(lambda e, g=g: e.matmul(psum[:, (g + 1) * BANK:(g + 1) * BANK + SEQ],
                                                 wqkv[:, g * D:(g + 1) * D], xt[:], start=True, stop=True), p_g)
        for h in range(HALVES):
            done = pe.do(lambda e, h=h: e.matmul(psum[:, (6 + h) * BANK:(6 + h) * BANK + D],
                                                 xt[:, h * P:(h + 1) * P], wqkv[:, (SETS + 1) * D:(SETS + 2) * D],
                                                 start=True, stop=True), p_g)
        act.wait(done)
        for g in range(SETS + 1):
            act.do(lambda e, g=g: e.copy(qk[:, g, :], psum[:, (g + 1) * BANK:(g + 1) * BANK + SEQ]), a_g)
        for h in range(HALVES):
            done = act.do(lambda e, h=h: e.copy(vt[:, h, :], psum[:, (6 + h) * BANK:(6 + h) * BANK + D]), a_g)
        sync.wait(done)
        for g in range(SETS):
            sync.dma(lambda e, g=g, heads=heads: e.dma_start(dq[heads, g], qk[:, g, :]), s_g)
        sync.dma(lambda e, heads=heads: e.dma_start(dk[heads], qk[:, SETS, :]), s_g)
        for h in range(HALVES):
            wrote = sync.dma(lambda e, h=h, heads=heads: e.dma_start(
                dv[heads, h * P:(h + 1) * P, :].rearrange("n t d -> t n d"),
                vt[:, h, :].rearrange("t (n d) -> t n d", d=HD)), s_g)
    pe.wait(wrote)
    act.wait(wrote)
    dve.wait(wrote, mask_here)
    sync.wait(wrote)

    l_in, l_p, l_v, l_a, l_out = (sig(n) for n in ("loop_loads", "loop_tensor", "loop_vector", "loop_scalar",
                                                   "loop_stores"))
    IN, PEN, VN, AN, OUTN = 16 * (2 + HALVES), 3, 5, 2, 16 * SETS

    def loop_sync(e):
        e.sem_inc(l_out.sem, 1)
        with e.Fori(0, BH) as i:
            e.wait_ge(l_out.sem, i * OUTN + 1)
            e.dma_start(q_h[:], dq[bass.ds(i, 1)].rearrange("a g d t -> d (a g) t")).then_inc(l_in.sem, 16)
            e.dma_start(k_h[:], dk[bass.ds(i, 1)].rearrange("a d t -> d (a t)")).then_inc(l_in.sem, 16)
            for h in range(HALVES):
                e.dma_start(v_h[:, h, :], dv[bass.ds(i, 1), h * P:(h + 1) * P].rearrange("a t d -> t (a d)"))\
                 .then_inc(l_in.sem, 16)
            e.wait_ge(l_v.sem, i * VN + VN)
            for g in range(SETS):
                e.dma_start(do[bass.ds(i, 1), g].rearrange("a (h t) d -> t (a h) d", h=HALVES),
                            o_h[:, g * HALVES:(g + 1) * HALVES, :]).then_inc(l_out.sem, 16)

    def loop_pe(e):
        with e.Fori(0, BH) as i:
            e.wait_ge(l_in.sem, i * IN + IN)
            for g in range(SETS):
                for h in range(HALVES):
                    last = e.matmul(psum[:, g * BANK + h * SEQ:g * BANK + (h + 1) * SEQ], q_h[:, g, h * P:(h + 1) * P],
                                    k_h[:], start=True, stop=True)
            last.then_inc(l_p.sem, 1)
            e.wait_ge(l_v.sem, i * VN + 4)
            for g in range(SETS):
                for k in range(HALVES):
                    for h in range(HALVES):
                        at = (SETS + g) * BANK + (k * HALVES + h) * P
                        last = e.transpose(psum[:, at:at + P], weights[:, g * HALVES + h, k * P:(k + 1) * P], eye[:])
            last.then_inc(l_p.sem, 1)
            e.wait_ge(l_a.sem, i * AN + 2)
            for g in range(SETS):
                for h in range(HALVES):
                    for k in range(HALVES):
                        at = (k * HALVES + h) * P
                        last = e.matmul(psum[:, (g * HALVES + h) * HD:(g * HALVES + h + 1) * HD],
                                        turned_w[:, g, at:at + P], v_h[:, k, :], start=(k == 0), stop=(k == HALVES - 1))
            last.then_inc(l_p.sem, 1)

    def loop_dve(e):
        with e.Fori(0, BH) as i:
            e.wait_ge(l_p.sem, i * PEN + 1)
            for g in range(SETS):
                last = e.tensor_tensor(raw[:, g], psum[:, g * BANK:g * BANK + HALVES * SEQ].rearrange(
                    "p (h k) -> p h k", k=SEQ), masked[:], ALU.add)
            last.then_inc(l_v.sem, 1)
            e.wait_ge(l_v.sem, i * VN + 1)
            e.reduce_max(peak[:], raw[:].rearrange("p g h k -> p (g h) k"), AX_X).then_inc(l_v.sem, 1)
            e.wait_ge(l_v.sem, i * VN + 2)
            e.tensor_scalar(shift[:], peak[:], -SCALE, None, ALU.mult).then_inc(l_v.sem, 1)
            e.wait_ge(l_a.sem, i * AN + 1)
            e.reciprocal(inv[:], total[:]).then_inc(l_t.sem, 1)
            e.wait_ge(l_t.sem, i + 1)
            e.tensor_tensor(weights[:], weights[:], inv[:].rearrange("p (n a) -> p n a", a=1).to_broadcast(
                [P, SETS * HALVES, SEQ]), ALU.mult).then_inc(l_v.sem, 1)
            e.wait_ge(l_p.sem, i * PEN + 3)
            e.tensor_copy(o_h[:], psum[:, 0:SETS * HALVES * HD].rearrange("p (n d) -> p n d", d=HD))\
             .then_inc(l_v.sem, 1)

    l_t = sig("loop_inverse")

    def loop_act(e):
        with e.Fori(0, BH) as i:
            e.wait_ge(l_v.sem, i * VN + 3)
            for n in range(SETS * HALVES):
                last = e.activation(weights[:, n, :], raw[:, n // HALVES, n % HALVES, :], ACT.Exp, scale=SCALE,
                                    bias=shift[:, n:n + 1], accum_out=total[:, n:n + 1])
            last.then_inc(l_a.sem, 1)
            e.wait_ge(l_p.sem, i * PEN + 2)
            e.copy(turned_w[:].rearrange("p g n -> p (g n)"), psum[:, SETS * BANK:2 * SETS * BANK]).then_inc(l_a.sem, 1)

    tails = [Stream(n) for n in ("tensor", "scalar", "vector", "sync")]
    tpe, tact, tdve, tsync = tails
    stored = (l_out, BH * OUTN + 1)
    tsync.wait(stored)
    tpe.wait(stored)
    added = None
    for t in range(TILES):
        b, h = divmod(t, HALVES)
        tsync.wait(added)
        for n in range(HEADS):
            got = tsync.dma(lambda e, n=n, b=b, h=h: e.dma_start(
                o_tok[:].rearrange("p (g n d) -> p g n d", g=SETS, d=HD)[:, :, n, :],
                do[b * HEADS + n, :, h * P:(h + 1) * P, :].rearrange("g t d -> t g d")), s_g)
        tpe.wait(got)
        for g in range(SETS):
            done = tpe.do(lambda e, g=g: e.transpose(psum[:, g * P:(g + 1) * P], o_tok[:, g * D:(g + 1) * D], eye[:]), p_g)
        tact.wait(done)
        done = tact.do(lambda e: e.copy(o_rows[:], psum[:, 0:SETS * P]), a_g)
        tpe.wait(done)
        for g in range(SETS):
            done = tpe.do(lambda e, g=g: e.matmul(psum[:, BANK:BANK + D], o_rows[:, g * P:(g + 1) * P], wproj[:, g, :],
                                                  start=(g == 0), stop=(g == SETS - 1)), p_g)
        tdve.wait(done)
        added = tdve.do(lambda e, t=t: e.tensor_tensor(attended[:, t, :], psum[:, BANK:BANK + D], stream[:, t, :],
                                                       ALU.add), v_g)
    bodies = []
    for head, loop, tail in ((pe, loop_pe, tpe), (act, loop_act, tact), (dve, loop_dve, tdve),
                             (None, None, None), (sync, loop_sync, tsync)):
        def body(e, head=head, loop=loop, tail=tail):
            if head is not None:
                head.play(e)
                loop(e)
                tail.play(e)
            e.wait_ge(added[0].sem, added[1])
        bodies.append(body)
    return bodies


def build(nc, dr, out):
    with ExitStack() as ctx:
        def sb(name, shape, dt=F32):
            return ctx.enter_context(nc.sbuf_tensor(name, shape, dt))

        def sig(name):
            return Signal(ctx, nc, name)

        pe, act, dve, pool, sync = (Stream(n) for n in ("tensor", "scalar", "vector", "gpsimd", "sync"))
        psum = ctx.enter_context(nc.psum_tensor("psum", [P, 8 * BANK], F32))

        stream = sb("stream", [P, TILES, D])
        attended = sb("attended", [P, TILES, D])
        good = sb("good", [P, BATCH + 1])
        bad = sb("bad", [1, 1], mybir.dt.int32)
        normed = sb("normed", [P, TILES, D])
        stats = sb("stats", [P, TILES, 6])
        meanvar = sb("meanvar", [P, TILES, 2])
        rstd = sb("rstd", [P, TILES])
        vareps = sb("vareps", [P, TILES])
        minus_half = sb("minus_half", [P, TILES])
        eye = sb("eye", [P, P])
        ramp = sb("ramp", [P, SEQ])
        keep = sb("keep", [P, 2 * P])
        lanes = sb("lanes", [P, LANES])
        expert_no = sb("expert_no", [P, FFN_TILES, EXPERTS])
        wg = sb("wg", [P, EXPERTS])
        bg = sb("bg", [P, EXPERTS])
        w1 = sb("w1", [P, EXPERTS, HIDDEN])
        b1 = sb("b1", [P, EXPERTS * HBLK])
        w2 = sb("w2", [P, EXPERTS * HBLK, D])
        b2 = sb("b2", [EXPERTS, D])
        wqkv = sb("wqkv", [P, (SETS + 2) * D])
        wproj = sb("wproj", [P, SETS, D])

        s_const, s_small, s_dft, s_expw, s_attw = (sig(n) for n in (
            "landed_consts", "landed_small", "landed_dft", "landed_expert_weights", "landed_attn_weights"))
        s_x = [sig(f"landed_x{i}") for i in range(CONV_CHUNKS)]
        s_out = sig("landed_out")
        v_ln, g_ln = sig("vector_ln"), sig("gpsimd_ln")

        def load(dst, src, signal):
            return sync.dma(lambda e: e.dma_start(dst, src), signal)

        x_tiles = dr["L0_attn_a_u"].rearrange("b (h p) m -> p (b h) m", p=P)
        out_tiles = out.rearrange("b (h p) m -> p (b h) m", p=P)
        conv_ctx = ExitStack()

        def csb(name, shape, dt=F32):
            return conv_ctx.enter_context(nc.sbuf_tensor(name, shape, dt))

        a_log, c_re = csb("a_log", [P, STATES]), csb("c_re", [P, STATES])
        log_dt, skip_d = csb("log_dt", [P, 1]), csb("skip_d", [P, 1])
        forward = csb("forward", [P, HALVES, 4 * P])
        taps = csb("taps", [P, HALVES, 5 * P])
        inverse = csb("inverse", [P, 4, SEQ])
        load(a_log[:], dr["L0_attn_a_A_log"].rearrange("(a n) -> a n", a=1).to_broadcast([P, STATES]), s_small)
        load(log_dt[:], dr["L0_attn_a_log_dt"].rearrange("(p a) -> p a", a=1), s_small)
        load(c_re[:], dr["L0_attn_a_C_re"], s_small)
        load(skip_d[:], dr["L0_attn_a_D"].rearrange("(p a) -> p a", a=1), s_small)
        small_here = load(ramp[:], dr["c_ramp"], s_small)
        tiles_per = CONV_BATCHES * HALVES
        x_here = [load(stream[:, i * tiles_per:(i + 1) * tiles_per, :],
                       x_tiles[:, i * tiles_per:(i + 1) * tiles_per, :], s_x[i]) for i in range(CONV_CHUNKS)]
        load(eye[:], dr["c_eye"], s_dft)
        load(taps[:], dr["c_taps"], s_dft)
        load(forward[:], dr["c_forward"], s_dft)
        dft_here = load(inverse[:], dr["c_inverse"], s_dft)
        load(wg[:], dr["L0_ffn_Wg"], s_expw)
        load(bg[:], dr["L0_ffn_bg"].rearrange("(a n) -> a n", a=1).to_broadcast([P, EXPERTS]), s_expw)
        load(expert_no[:], dr["c_expert"], s_expw)
        load(b1[:], dr["b1_cols"], s_expw)
        load(b2[:], dr["L0_ffn_b2"], s_expw)
        load(w1[:], dr["L0_ffn_W1"].rearrange("e d h -> d e h"), s_expw)
        expw_here = load(w2[:], dr["L0_ffn_W2"].rearrange("e (k p) d -> p (e k) d", p=P), s_expw)
        load(keep[:], dr["c_keep"], s_attw)
        load(lanes[:], dr["c_lanes"], s_attw)
        load(wqkv[:], dr["w_attn_cols"], s_attw)
        attw_here = load(wproj[:], dr["w_proj_rows"], s_attw)

        pow_ready = pool.do(lambda e: e.memset(minus_half[:], -0.5), g_ln)

        def layer_norm(x, t0, n, ready):
            dve.wait(*ready)
            for t in range(t0, t0 + n):
                stats_done = dve.do(lambda e, t=t: e.bn_stats(stats[:, t, :], x[:, t, :]), v_ln)
            dve.wait(stats_done)
            for t in range(t0, t0 + n):
                agg = dve.do(lambda e, t=t: e.bn_aggr(meanvar[:, t, :], stats[:, t, :]), v_ln)
            pool.wait(agg, pow_ready)
            eps_done = pool.do(lambda e: e.tensor_scalar(vareps[:, t0:t0 + n], meanvar[:, t0:t0 + n, 1], EPS, None,
                                                         ALU.add), g_ln)
            pool.wait(eps_done)
            rstd_done = pool.do(lambda e: e.tensor_tensor(rstd[:, t0:t0 + n], vareps[:, t0:t0 + n],
                                                          minus_half[:, t0:t0 + n], ALU.pow), g_ln)
            yield
            dve.wait(rstd_done)
            for t in range(t0, t0 + n):
                done = dve.do(lambda e, t=t: e.tensor_scalar(normed[:, t, :], x[:, t, :], meanvar[:, t, 0:1],
                                                             rstd[:, t:t + 1], ALU.subtract, ALU.mult), v_ln)
            yield done

        def last(gen):
            got = None
            for got in gen:
                pass
            return got

        a_k, v_k, p_k = sig("scalar_taps"), sig("vector_taps"), sig("tensor_taps")
        v_y, g_y, p_f, p_y = sig("vector_conv"), sig("gpsimd_conv"), sig("tensor_forward"), sig("tensor_inverse")
        CHAINS, ERING, LN_AT = 4, 8, (32,)
        neg_a, dt, z = csb("neg_a", [P, STATES]), csb("dt", [P, 1]), csb("z", [P, STATES])
        decay = csb("decay", [P, ERING, SEQ])
        chain = csb("chain", [P, CHAINS, SEQ])
        ktap = csb("ktap", [P, HALVES, D])
        khat = csb("khat", [P, 5, D])

        act.wait(small_here)
        act.do(lambda e: e.activation(neg_a[:], a_log[:], ACT.Exp), a_k)
        exps_done = act.do(lambda e: e.activation(dt[:], log_dt[:], ACT.Exp), a_k)
        dve.wait(exps_done)
        z_done = dve.do(lambda e: e.tensor_scalar(z[:], neg_a[:], dt[:, 0:1], -1.0, ALU.mult, ALU.mult), v_k)
        act.wait(z_done)
        dve.wait(small_here)
        mac_done = []
        ln_ready = [last(layer_norm(stream, 0, tiles_per, [x_here[0]]))]
        for n in range(STATES):
            if n >= ERING:
                act.wait(mac_done[n - ERING])
            decayed = act.do(lambda e, n=n: e.activation(decay[:, n % ERING, :], ramp[:], ACT.Exp,
                                                         scale=z[:, n:n + 1]), a_k)
            if n in LN_AT:
                ch = len(ln_ready)
                ln_ready.append(last(layer_norm(stream, ch * tiles_per, tiles_per, [x_here[ch]])))
            dve.wait(decayed)
            c = n % CHAINS
            if n < CHAINS:
                mac_done.append(dve.do(lambda e, n=n, c=c: e.tensor_scalar(
                    chain[:, c, :], decay[:, n % ERING, :], c_re[:, n:n + 1], None, ALU.mult), v_k))
            else:
                dve.wait(mac_done[n - CHAINS])
                mac_done.append(dve.do(lambda e, n=n, c=c: e.scalar_tensor_tensor(
                    out=chain[:, c, :], in0=decay[:, n % ERING, :], scalar=c_re[:, n:n + 1],
                    in1=chain[:, c, :], op0=ALU.mult, op1=ALU.add), v_k))
        dve.wait(mac_done[-1])
        summed = dve.do(lambda e: e.tensor_tensor(chain[:, 0:2, :], chain[:, 0:2, :], chain[:, 2:4, :], ALU.add), v_k)
        dve.wait(summed)
        summed = dve.do(lambda e: e.tensor_tensor(chain[:, 0, :], chain[:, 0, :], chain[:, 1, :], ALU.add), v_k)
        dve.wait(summed)
        taps_done = dve.do(lambda e: e.tensor_tensor(chain[:, 0, 0:1], chain[:, 0, 0:1], skip_d[:], ALU.add), v_k)

        prod = csb("prod", [P, 2, 4, BANK])
        yhat = csb("yhat", [P, 2, 4, BANK])
        conv_done = []
        fb, ib, kb = Banks(psum, [0, 1, 2, 3]), Banks(psum, [4, 5, 6, 7]), Banks(psum, [6, 7])
        yhat_read, prod_read = [None, None], [None, None]
        fwd, y_done, inv_done = {}, {}, {}

        def forward_chunk(ch):
            un = normed[:, ch * tiles_per:(ch + 1) * tiles_per, :].rearrange("p (b h) m -> p h b m", h=HALVES)
            pe.wait(ln_ready[ch])
            for i in (0, 2, 1, 3):
                bank, before, free = fb.take()
                pe.wait(*before)
                for h in range(HALVES):
                    done = pe.do(lambda e, i=i, h=h, bank=bank, un=un: e.matmul(
                        bank, forward[:, h, i * P:(i + 1) * P], un[:, h], start=(h == 0), stop=(h == HALVES - 1)),
                        p_f if h == HALVES - 1 else None)
                fwd[ch, i] = (bank, free, done)

        def products(ch):
            s = ch % 2
            y_done[ch] = []
            for f in range(2):
                (re, re_free, re_done), (im, im_free, im_done) = fwd[ch, f], fwd[ch, 2 + f]
                dve.wait(re_done, im_done, prod_read[f])
                last_cos = 4 if f == 0 else 1
                for n, (src, free, k) in enumerate(((re, re_free, f), (im, im_free, 2 + f),
                                                    (re, re_free, 2 + f), (im, im_free, last_cos))):
                    done = dve.do(lambda e, n=n, src=src, k=k, f=f: e.tensor_tensor(
                        prod[:, f, n, :].rearrange("p (b m) -> p b m", m=D), src.rearrange("p (b m) -> p b m", m=D),
                        khat[:, k:k + 1, :].to_broadcast([P, CONV_BATCHES, D]), ALU.mult), v_y)
                    if n >= 2:
                        free.append(done)
                    if n == 1:
                        both = done
                pool.wait(both, yhat_read[s])
                eng_re = pool.do(lambda e, s=s, f=f: e.tensor_tensor(yhat[:, s, f, :], prod[:, f, 0, :], prod[:, f, 1, :],
                                                                     ALU.subtract), g_y)
                pool.wait(done)
                eng_im = pool.do(lambda e, s=s, f=f: e.tensor_tensor(yhat[:, s, 2 + f, :], prod[:, f, 2, :],
                                                                     prod[:, f, 3, :], ALU.add), g_y)
                prod_read[f] = eng_im
                y_done[ch] += [eng_re, eng_im]

        def inverse_chunk(ch):
            s = ch % 2
            pe.wait(*y_done[ch])
            for h in range(HALVES):
                bank, before, free = ib.take()
                pe.wait(*before)
                for i in range(4):
                    done = pe.do(lambda e, i=i, h=h, s=s, bank=bank: e.matmul(
                        bank, inverse[:, i, h * P:(h + 1) * P], yhat[:, s, i, :], start=(i == 0), stop=(i == 3)),
                        p_y if i == 3 else None)
                yhat_read[s] = done
                inv_done[ch, h] = (bank, free, done)

        def residual(ch):
            for h in range(HALVES):
                bank, free, done = inv_done[ch, h]
                dve.wait(done)
                half = stream[:, ch * tiles_per:(ch + 1) * tiles_per, :].rearrange("p (b h) m -> p h b m", h=HALVES)[:, h]
                added = dve.do(lambda e, bank=bank, half=half: e.tensor_tensor(
                    half, bank.rearrange("p (b m) -> p b m", m=D), half, ALU.add), v_y)
                free.append(added)
            conv_done.append(added)

        pe.wait(dft_here)
        forward_chunk(0)
        pe.wait(taps_done, dft_here)
        bank, before, free = kb.take()
        for h in range(HALVES):
            turned = pe.do(lambda e, h=h, bank=bank: e.transpose(bank[:, h * P:(h + 1) * P],
                                                                 chain[:, 0, h * P:(h + 1) * P], eye[:]), p_k)
        act.wait(turned)
        ktap_done = act.do(lambda e, bank=bank: e.copy(ktap[:], bank[:, 0:HALVES * P]), a_k)
        free.append(ktap_done)
        pe.wait(ktap_done)
        for lo, hi in ((0, 4), (4, 5)):
            bank, before, free = kb.take()
            pe.wait(*before)
            for i in range(lo, hi):
                for h in range(HALVES):
                    done = pe.do(lambda e, i=i, h=h, lo=lo, bank=bank: e.matmul(
                        bank[:, (i - lo) * P:(i - lo + 1) * P], taps[:, h, i * P:(i + 1) * P], ktap[:, h, :],
                        start=(h == 0), stop=(h == HALVES - 1)), p_k if h == HALVES - 1 else None)
            act.wait(done)
            khat_done = act.do(lambda e, lo=lo, hi=hi, bank=bank: e.copy(khat[:, lo:hi, :], bank[:, 0:(hi - lo) * P]),
                               a_k)
            free.append(khat_done)

        for taps_bank, inverse_bank in zip(kb.free, ib.free[2:]):
            inverse_bank += taps_bank
        dve.wait(khat_done)
        for ch in range(CONV_CHUNKS):
            products(ch)
            if len(ln_ready) < CONV_CHUNKS:
                n = len(ln_ready)
                ln_ready.append(last(layer_norm(stream, n * tiles_per, tiles_per, [x_here[n]])))
            if ch + 1 < CONV_CHUNKS:
                forward_chunk(ch + 1)
            inverse_chunk(ch)
            if ch:
                residual(ch - 1)
        residual(CONV_CHUNKS - 1)
        conv_inverse_done = inv_done[CONV_CHUNKS - 1, HALVES - 1][2]
        conv_ctx.close()
        conv_over = [conv_done[-1], conv_inverse_done]

        CH = FFN_TILES * P
        p_e, a_e, v_e = sig("tensor_experts"), sig("scalar_experts"), sig("vector_experts")

        def moe(tag, x, ready_of_tile, after_chunk, after_norm, fence):
            own = ExitStack()

            def msb(name, shape, dt=F32):
                return own.enter_context(nc.sbuf_tensor(f"{name}_{tag}", shape, dt))

            xt = msb("xt", [P, 2, CH])
            logits = msb("logits", [P, 2, FFN_TILES, EXPERTS])
            top = msb("top", [P, 2, FFN_TILES, 8])
            top_at = msb("top_at", [P, 2, FFN_TILES, 8], U32)
            top_no = msb("top_no", [P, 2, FFN_TILES, 2])
            gap = msb("gap", [P, 2, FFN_TILES])
            wpair = msb("wpair", [P, 2, 2, FFN_TILES])
            pick = msb("pick", [P, 2, 2, FFN_TILES, EXPERTS])
            comb = msb("comb", [P, 2, FFN_TILES, EXPERTS])
            comb_t = msb("comb_t", [EXPERTS, 2, CH])
            hidden = msb("hidden", [P, 3, HBLK, CH])
            own.close()
            later = []
            misc, hb, yb = Banks(psum, [6, 7]), Banks(psum, [0, 1, 2, 3]), Banks(psum, [4, 5])
            for bb in (misc, hb, yb):
                for f in bb.free:
                    f.extend(fence)
            for s_ in (act, dve, pool):
                s_.wait(*fence)
            xt_free, comb_free, combt_free, hid_free = [None] * 2, [None] * 2, [None] * 2, [None] * 3
            state = {}

            def prologue(ch):
                s, t0 = ch % 2, ch * FFN_TILES
                gen = layer_norm(x, t0, FFN_TILES, [ready_of_tile(t) for t in range(t0, t0 + FFN_TILES)])
                next(gen)
                yield
                normed_done = last(gen)
                yield
                bank, before, free = misc.take()
                pe.wait(normed_done, *before)
                for i in range(FFN_TILES):
                    done = pe.do(lambda e, i=i, bank=bank: e.transpose(bank[:, i * P:(i + 1) * P], normed[:, t0 + i, :],
                                                                       eye[:]), p_e if i == FFN_TILES - 1 else None)
                act.wait(done, xt_free[s])
                xt_done = act.do(lambda e, bank=bank: e.copy(xt[:, s, :], bank), a_e)
                free.append(xt_done)
                yield
                bank, before, free = misc.take()
                pe.wait(xt_done, *before)
                for i in range(FFN_TILES):
                    done = pe.do(lambda e, i=i, bank=bank: e.matmul(bank[:, i * EXPERTS:(i + 1) * EXPERTS],
                                                                    xt[:, s, i * P:(i + 1) * P], wg[:],
                                                                    start=True, stop=True),
                                 p_e if i == FFN_TILES - 1 else None)
                dve.wait(done)
                lg = logits[:, s]
                lg_done = dve.do(lambda e, bank=bank: e.tensor_tensor(
                    lg, bank[:, 0:FFN_TILES * EXPERTS].rearrange("p (t e) -> p t e", e=EXPERTS),
                    bg[:].rearrange("p (a e) -> p a e", a=1).to_broadcast([P, FFN_TILES, EXPERTS]), ALU.add), v_e)
                free.append(lg_done)
                dve.wait(lg_done)
                for i in range(FFN_TILES):
                    tops = dve.do(lambda e, i=i: e.max(top[:, s, i, :], logits[:, s, i, :]), v_e)
                dve.wait(tops)
                for i in range(FFN_TILES):
                    found = dve.do(lambda e, i=i: e.max_index(top_at[:, s, i, :], top[:, s, i, :], logits[:, s, i, :]),
                                   v_e)
                gap_done = dve.do(lambda e: e.tensor_tensor(gap[:, s, :], top[:, s, :, 1], top[:, s, :, 0],
                                                            ALU.subtract), v_e)
                act.wait(gap_done)
                ex_done = act.do(lambda e: e.activation(gap[:, s, :], gap[:, s, :], ACT.Exp), a_e)
                yield
                dve.wait(found)
                no_done = dve.do(lambda e: e.tensor_copy(top_no[:, s], top_at[:, s, :, 0:2]), v_e)
                dve.wait(ex_done)
                den = dve.do(lambda e: e.tensor_scalar(wpair[:, s, 1, :], gap[:, s, :], 1.0, None, ALU.add), v_e)
                dve.wait(den)
                w0 = dve.do(lambda e: e.reciprocal(wpair[:, s, 0, :], wpair[:, s, 1, :]), v_e)
                dve.wait(no_done, w0)
                w1_ = dve.do(lambda e: e.tensor_tensor(wpair[:, s, 1, :], wpair[:, s, 0, :], gap[:, s, :], ALU.mult), v_e)
                for k in range(2):
                    picked = dve.do(lambda e, k=k: e.tensor_tensor(
                        pick[:, s, k], expert_no[:], top_no[:, s, :, k:k + 1].to_broadcast([P, FFN_TILES, EXPERTS]),
                        ALU.is_equal), v_e)
                dve.wait(w1_, picked)
                for k in range(2):
                    scaled = dve.do(lambda e, k=k: e.tensor_tensor(
                        pick[:, s, k], pick[:, s, k],
                        wpair[:, s, k, :].rearrange("p (t a) -> p t a", a=1).to_broadcast([P, FFN_TILES, EXPERTS]),
                        ALU.mult), v_e)
                dve.wait(scaled, comb_free[s])
                comb_done = dve.do(lambda e: e.tensor_tensor(comb[:, s], pick[:, s, 0], pick[:, s, 1], ALU.add), v_e)
                yield
                bank, before, free = misc.take()
                pe.wait(comb_done, *before)
                for i in range(FFN_TILES):
                    done = pe.do(lambda e, i=i, bank=bank: e.transpose(bank[0:EXPERTS, i * P:(i + 1) * P],
                                                                       comb[:, s, i, :], eye[:]),
                                 p_e if i == FFN_TILES - 1 else None)
                act.wait(done, combt_free[s])
                ct_done = act.do(lambda e, bank=bank: e.copy(comb_t[:, s, :], bank[0:EXPERTS, :]), a_e)
                free.append(ct_done)
                yield
                bank, before, free = misc.take()
                pe.wait(ct_done, *before)
                for i in range(FFN_TILES):
                    done = pe.do(lambda e, i=i, bank=bank: e.matmul(bank[:, i * P:(i + 1) * P],
                                                                    comb_t[:, s, i * P:(i + 1) * P], b2[:],
                                                                    start=True, stop=True),
                                 p_e if i == FFN_TILES - 1 else None)
                combt_free[s] = done
                dve.wait(done, normed_done)
                base = dve.do(lambda e, bank=bank: e.tensor_tensor(
                    x[:, t0:t0 + FFN_TILES, :], bank.rearrange("p (t m) -> p t m", m=D),
                    x[:, t0:t0 + FFN_TILES, :], ALU.add), v_e)
                free.append(base)
                state[ch] = (xt_done, base)

            def up(ch, e_):
                s, r = ch % 2, (ch * EXPERTS + e_) % 3
                for k in range(HBLK):
                    bank, before, free = hb.take()
                    pe.wait(state[ch][0], *before)
                    done = pe.do(lambda e, k=k, bank=bank: e.matmul(bank, w1[:, e_, k * P:(k + 1) * P], xt[:, s, :],
                                                                    start=True, stop=True), p_e)
                    act.wait(done, hid_free[r])
                    relu = act.do(lambda e, k=k, bank=bank: e.activation(
                        hidden[:, r, k, :], bank, ACT.Relu, bias=b1[:, e_ * HBLK + k:e_ * HBLK + k + 1]), a_e)
                    free.append(relu)
                if e_ == EXPERTS - 1:
                    xt_free[s] = done
                return relu

            def down(ch, e_, relu):
                s, r, t0 = ch % 2, (ch * EXPERTS + e_) % 3, ch * FFN_TILES
                bank, before, free = yb.take()
                pe.wait(relu, *before)
                for i in range(FFN_TILES):
                    for k in range(HBLK):
                        done = pe.do(lambda e, i=i, k=k, bank=bank: e.matmul(
                            bank[:, i * P:(i + 1) * P], hidden[:, r, k, i * P:(i + 1) * P], w2[:, e_ * HBLK + k, :],
                            start=(k == 0), stop=(k == HBLK - 1)),
                            p_e if i == FFN_TILES - 1 and k == HBLK - 1 else None)
                hid_free[r] = done
                dve.wait(done, state[ch][1], state.get((ch, "acc")))
                for i in range(FFN_TILES):
                    acc = dve.do(lambda e, i=i, bank=bank: e.scalar_tensor_tensor(
                        out=x[:, t0 + i, :], in0=bank[:, i * P:(i + 1) * P], scalar=comb[:, s, i, e_:e_ + 1],
                        in1=x[:, t0 + i, :], op0=ALU.mult, op1=ALU.add), v_e)
                free.append(acc)
                state[ch, "acc"] = acc
                if e_ == EXPERTS - 1:
                    comb_free[s] = acc
                    after_chunk(ch, acc)
                    later[:] = [after_norm(ch, acc)] if after_norm else []

            pe.wait(expw_here)
            dve.wait(expw_here)
            act.wait(expw_here)
            for _ in prologue(0):
                pass
            pending = None
            for ch in range(FFN_CHUNKS):
                ahead = prologue(ch + 1) if ch + 1 < FFN_CHUNKS else iter(())
                for e_ in range(EXPERTS):
                    relu = up(ch, e_)
                    if pending:
                        down(*pending)
                    pending = (ch, e_, relu)
                    next(ahead, None)
                    for gen in later:
                        next(gen, None)
                for _ in ahead:
                    pass
            down(*pending)
            for gen in later:
                last(gen)
            return [acc_ for acc_ in (state[FFN_CHUNKS - 1, "acc"],)]

        ffn1_normed = {}

        def norm_for_attention(ch, acc):
            for ev in layer_norm(stream, ch * FFN_TILES, FFN_TILES, [acc]):
                ffn1_normed[ch] = ev
                yield

        fence = moe("first", stream, lambda t: conv_done[t // tiles_per], lambda ch, acc: None, norm_for_attention, conv_over)

        ROWS = 2 * LANES * HD
        scratch = nc.dram_tensor("qk_parts", [2, ROWS, QUADS, SETS + 1, SEQ], F16, kind="Internal").ap()
        att = ExitStack()

        def asb(name, shape, dt=F32):
            return att.enter_context(nc.sbuf_tensor(name, shape, dt))

        at_x = asb("at_x", [P, 2, SEQ])
        parts = asb("parts", [P, 2, 2, SETS + 1, SEQ], F16)
        qstack = asb("qstack", [P, 2, QUADS, SETS + 1, SEQ], F16)
        kfull = asb("kfull", [P, 2, QUADS, SEQ], F16)
        kstack = asb("kstack", [P, 2, LANES, QUADS, SEQ], F16)
        vstack = asb("vstack", [P, 2, HALVES, HEADS, SLOT])
        prob = asb("prob", [P, 3, LANES, UNIT])
        o_sb = asb("o_sb", [P, 2, BANK])
        o_tok = asb("o_tok", [P, 2, HALVES, SETS, D])
        rden = asb("rden", [P, BATCH, QUADS * PAIRS, 2 * 2 * LANES])
        in_range = asb("in_range", [P, QUADS * PAIRS * 2 * 2 * LANES])
        o_rows = asb("o_rows", [P, 2, BANK])
        p_a, a_a, v_a, g_a = sig("tensor_attn"), sig("scalar_attn"), sig("vector_attn"), sig("gpsimd_attn")
        s_parts = [sig(f"landed_parts{i}") for i in range(2)]
        s_stack = [sig(f"landed_stack{i}") for i in range(2)]

        misc, ob = Banks(psum, [6, 7]), Banks(psum, [4, 5])
        for bb in (misc, ob):
            for f in bb.free:
                f.extend(fence)
        score_banks = [psum[:, 2 * i * BANK:2 * i * BANK + UNIT] for i in range(2)]
        score_free = [list(fence), list(fence)]
        pool.wait(*conv_over, *fence)
        pool.do(lambda e: e.memset(vstack[:], 0.0), g_a)
        zeroed = (g_a, g_a.value)
        pool.wait(zeroed)
        zeroed = pool.do(lambda e: e.memset(vstack[:, :, :, :, HD:HD + 1], 1.0), g_a)
        for q_ in (pe, act, dve):
            q_.wait(*fence, attw_here)
        slot_free = {"x": [None] * 2, "parts": [None] * 2, "stack": [None] * 2, "kfull": [None] * 2, "v": [None] * 2,
                     "scratch": [None] * 2, "otok": [None] * 2}
        ready = {}

        def attn_prologue(b):
            s = b % 2
            normed_done = ffn1_normed[HALVES * b // FFN_TILES]
            bank, before, free = misc.take()
            pe.wait(normed_done, *before)
            for h in range(HALVES):
                done = pe.do(lambda e, h=h, bank=bank: e.transpose(bank[:, h * P:(h + 1) * P],
                                                                   normed[:, HALVES * b + h, :], eye[:]),
                             p_a if h == HALVES - 1 else None)
            act.wait(done, slot_free["x"][s])
            x_done = act.do(lambda e, bank=bank: e.copy(at_x[:, s, :], bank[:, 0:SEQ]), a_a)
            free.append(x_done)
            yield
            for g0 in range(0, SETS + 1, 2):
                n = min(2, SETS + 1 - g0)
                bank, before, free = misc.take()
                pe.wait(x_done, *before)
                for g in range(g0, g0 + n):
                    done = pe.do(lambda e, g=g, g0=g0, bank=bank: e.matmul(
                        bank[:, (g - g0) * SEQ:(g - g0 + 1) * SEQ], wqkv[:, g * D:(g + 1) * D], at_x[:, s, :],
                        start=True, stop=True), p_a if g == g0 + n - 1 else None)
                act.wait(done, slot_free["parts"][s])
                src = bank[:, 0:n * SEQ].rearrange("p (g t) -> p g t", t=SEQ)
                hi = act.do(lambda e, g0=g0, n=n, src=src: e.copy(parts[:, s, 0, g0:g0 + n, :], src), a_a)
                dve.wait(hi)
                lo = dve.do(lambda e, g0=g0, n=n, src=src: e.tensor_tensor(
                    parts[:, s, 1, g0:g0 + n, :], src, parts[:, s, 0, g0:g0 + n, :], ALU.subtract), v_a)
                free.append(lo)
                yield
            sync.wait(lo, hi, slot_free["scratch"][s])
            for c in range(QUADS):
                wrote = sync.dma(lambda e, c=c: e.dma_start(
                    scratch[s].rearrange("(a r) c g t -> r a c (g t)", a=2)[:, :, c],
                    parts[c * SLOT:(c + 1) * SLOT, s].rearrange("r a g t -> r a (g t)")), s_parts[s])
            slot_free["parts"][s] = wrote
            sync.wait(wrote, slot_free["stack"][s], slot_free["kfull"][s])
            twice = scratch[s:s + 1].rearrange("a r c g t -> a r (c g t)").to_broadcast([2, ROWS, QUADS * (SETS + 1) * SEQ])
            sync.dma(lambda e: e.dma_start(qstack[:, s].rearrange("p c g t -> p (c g t)"), twice), s_stack[s])
            krows = scratch[s][:, :, SETS, :]
            half = ROWS // 2
            sync.dma(lambda e: e.dma_start(kfull[0:ROWS, s], krows), s_stack[s])
            sync.dma(lambda e: e.dma_start(kfull[ROWS:ROWS + half, s], krows[half:ROWS]), s_stack[s])
            stacked = sync.dma(lambda e: e.dma_start(kfull[ROWS + half:P, s], krows[0:half]), s_stack[s])
            slot_free["scratch"][s] = stacked
            yield
            bank, before, free = misc.take()
            pe.wait(*before)
            for h in range(HALVES):
                done = pe.do(lambda e, h=h, bank=bank: e.matmul(bank[:, h * P:(h + 1) * P],
                                                                at_x[:, s, h * P:(h + 1) * P],
                                                                wqkv[:, (SETS + 1) * D:(SETS + 2) * D],
                                                                start=True, stop=True),
                             p_a if h == HALVES - 1 else None)
            slot_free["x"][s] = done
            act.wait(done, zeroed, slot_free["v"][s])
            v_done = act.do(lambda e, bank=bank: e.copy(
                vstack[:, s, :, :, 0:HD].rearrange("p h n d -> p (h n) d"),
                bank[:, 0:HALVES * D].rearrange("p (n d) -> p n d", d=HD)), a_a)
            free.append(v_done)
            for _ in range(7):
                yield
            dve.wait(stacked, slot_free["stack"][s])
            for lane in range(LANES):
                spread = dve.do(lambda e, lane=lane: e.tensor_scalar(
                    kstack[:, s, lane].rearrange("p c t -> p (c t)"), kfull[:, s].rearrange("p c t -> p (c t)"),
                    lanes[:, lane:lane + 1], None, ALU.mult), v_a)
            slot_free["kfull"][s] = spread
            ready[b] = (spread, v_done, stacked)

        units = [0]
        POOL_LANES = (0, 2)
        probs_free = [None] * 3

        def scores(b, grp, lane):
            c, pair = divmod(grp, PAIRS)
            s, u, pb = b % 2, units[0] % 2, (b * QUADS * PAIRS + grp) % 3
            units[0] += 1
            qs = qstack[:, s, c, 2 * pair:2 * pair + 2, :]
            sbk = score_banks[u]
            pe.wait(ready[b][0], ready[b][2], *score_free[u])
            pe.do(lambda e: e.matmul(sbk[:, 0:2 * SEQ], kstack[:, s, lane, c, 0:P],
                                     qs.rearrange("p g (h q) -> p h g q", q=P), start=True, stop=True))
            done = pe.do(lambda e: e.matmul(sbk[:, 2 * SEQ:UNIT], kstack[:, s, lane, c, P:SEQ],
                                            qs[:, :, P:SEQ], start=True, stop=True), p_a)
            if grp == QUADS * PAIRS - 1 and lane == LANES - 1:
                slot_free["stack"][s] = done
            act.wait(done, probs_free[pb])
            ex = act.do(lambda e: e.activation(prob[:, pb, lane, :], sbk, ACT.Exp, scale=SCALE), a_a)
            score_free[u] = [ex]
            eng, sg = (pool, g_a) if lane in POOL_LANES else (dve, v_a)
            diag = prob[:, pb, lane, :].rearrange("p (n q) -> p n q", q=2 * P)[:, 0:3:2, :]
            eng.wait(ex)
            return eng.do(lambda e: e.tensor_tensor(
                diag, diag, keep[:].rearrange("p (a q) -> p a q", a=1).to_broadcast([P, 2, 2 * P]), ALU.mult), sg), ex

        def weighted(b, grp, half, masked, bank, before):
            c, _ = divmod(grp, PAIRS)
            s, pb = b % 2, (b * QUADS * PAIRS + grp) % 3
            if half == 0:
                pe.wait(*before, ready[b][1])
            for m, ex in masked:
                pe.wait(m)
            for lane in range(LANES):
                o = bank[SLOT * lane:SLOT * (lane + 1)]
                if half == 0:
                    done = pe.do(lambda e, lane=lane, o=o: e.matmul(
                        o, vstack[:, s, 0, c * LANES + lane, :], prob[:, pb, lane, 0:2 * SEQ],
                        start=True, stop=False))
                else:
                    done = pe.do(lambda e, lane=lane, o=o: e.matmul(
                        o[:, SEQ:2 * SEQ], vstack[:, s, 1, c * LANES + lane, :], prob[:, pb, lane, 2 * SEQ:UNIT],
                        start=False, stop=True), p_a if lane == LANES - 1 else None)
            if half == 1:
                probs_free[pb] = done
                if grp == QUADS * PAIRS - 1:
                    slot_free["v"][s] = done
            return done

        o_free = [None] * 2

        def turn_copy(b, grp, bank, free, done):
            r = grp % 2
            dve.wait(done, o_free[r])
            copied = dve.do(lambda e: e.tensor_copy(o_sb[:, r, :], bank), v_a)
            free.append(copied)
            return copied

        def turn(b, grp, copied):
            s, r = b % 2, grp % 2
            c, pair = divmod(grp, PAIRS)
            tb, before, tfree = misc.take()
            pe.wait(copied, *before)
            for n in range(4):
                done = pe.do(lambda e, n=n: e.transpose(tb[:, n * P:(n + 1) * P], o_sb[:, r, n * P:(n + 1) * P], eye[:]),
                             p_a if n == 3 else None)
            o_free[r] = done
            heads = tb.rearrange("p (n r) -> p n r", r=SLOT)
            rd = rden[:, b, grp, :].rearrange("p (n a) -> p n a", a=1)
            dve.wait(done)
            rec = dve.do(lambda e: e.reciprocal(rd, heads[:, :, HD:HD + 1]), v_a)
            dve.wait(rec, slot_free["otok"][s] if grp == 0 else None)
            nrm = dve.do(lambda e: e.tensor_tensor(
                o_tok[:, s, :, 2 * pair:2 * pair + 2, c * SLOT:(c + 1) * SLOT].rearrange("p h k (j d) -> p h k j d", d=HD),
                heads[:, :, 0:HD].rearrange("p (h k j) d -> p h k j d", h=HALVES, k=2),
                rd.rearrange("p (h k j) a -> p h k j a", h=HALVES, k=2).to_broadcast([P, HALVES, 2, LANES, HD]),
                ALU.mult), v_a)
            tfree.append(nrm)
            return nrm

        attn_done = {}
        rows_free = [None] * 2
        counted = [None]

        def attn_epilogue(b, nrm):
            s = b % 2
            rd = rden[:, b].rearrange("p g n -> p (g n)")
            dve.wait(nrm)
            low = dve.do(lambda e: e.tensor_scalar(in_range[:], rd, RDEN_MIN, None, ALU.is_ge), v_a)
            dve.wait(low)
            counted[0] = dve.do(lambda e: e.scalar_tensor_tensor(
                out=in_range[:], in0=rd, scalar=RDEN_MAX, in1=in_range[:], op0=ALU.is_le, op1=ALU.mult,
                accum_out=good[:, b:b + 1]), v_a)
            for h in range(HALVES):
                bank, before, free = misc.take()
                pe.wait(nrm, *before)
                for g in range(SETS):
                    done = pe.do(lambda e, g=g, h=h, bank=bank: e.transpose(
                        bank[:, g * P:(g + 1) * P], o_tok[:, s, h, g, :], eye[:]), p_a if g == SETS - 1 else None)
                act.wait(done, rows_free[h])
                copied = act.do(lambda e, h=h, bank=bank: e.copy(o_rows[:, h, :], bank), a_a)
                free.append(copied)
                if h == HALVES - 1:
                    slot_free["otok"][s] = done
                yield
                bank, before, free = misc.take()
                pe.wait(copied, *before)
                for g in range(SETS):
                    done = pe.do(lambda e, g=g, h=h, bank=bank: e.matmul(
                        bank[:, 0:D], o_rows[:, h, g * P:(g + 1) * P], wproj[:, g, :], start=(g == 0),
                        stop=(g == SETS - 1)), p_a if g == SETS - 1 else None)
                rows_free[h] = done
                t = HALVES * b + h
                dve.wait(done)
                added = dve.do(lambda e, t=t, bank=bank: e.tensor_tensor(attended[:, t, :], bank[:, 0:D],
                                                                         stream[:, t, :], ALU.add), v_a)
                free.append(added)
                attn_done[t] = added
                yield

        for _ in attn_prologue(0):
            pass
        NG = QUADS * PAIRS
        steps = [(b, g) for b in range(BATCH) for g in range(NG)]
        ahead, behind = iter(()), iter(())
        summed, copied_group, masked = None, None, None
        for n in range(len(steps) + 2):
            b, g = steps[n] if n < len(steps) else (None, None)
            back = steps[n - 1] if 1 <= n <= len(steps) else None
            if g == 0:
                for _ in ahead:
                    pass
                ahead = attn_prologue(b + 1) if b + 1 < BATCH else iter(())
            fresh = []
            if b is not None:
                fresh.append(scores(b, g, 0))
            next(ahead, None)
            if b is not None:
                fresh.append(scores(b, g, 1))
            if back:
                bank, before, free = ob.take()
                weighted(*back, 0, masked, bank, before)
            if b is not None:
                fresh.append(scores(b, g, 2))
            if copied_group:
                tb_, tg_, tc_ = copied_group
                nrm = turn(tb_, tg_, tc_)
                if tg_ == NG - 1:
                    for _ in behind:
                        pass
                    behind = attn_epilogue(tb_, nrm)
                copied_group = None
            if b is not None:
                fresh.append(scores(b, g, 3))
            next(ahead, None)
            if back:
                done = weighted(*back, 1, masked, bank, before)
                copied_group = (*back, turn_copy(*back, bank, free, done))
            next(behind, None)
            masked = fresh
        for _ in behind:
            pass
        dve.wait(counted[0])
        counted[0] = dve.do(lambda e: e.reduce_sum(good[:, BATCH:BATCH + 1], good[:, 0:BATCH], AX_X), v_a)
        bank, before, free = misc.take()
        pe.wait(counted[0], *before)
        turned = pe.do(lambda e: e.transpose(bank[0:1, 0:P], good[:, BATCH:BATCH + 1], eye[:]), p_a)
        dve.wait(turned)
        counted[0] = dve.do(lambda e: e.reduce_sum(good[0:1, 0:1], bank[0:1, 0:P], AX_X), v_a)
        dve.wait(counted[0])
        bad_known = dve.do(lambda e: e.tensor_scalar(bad[:], good[0:1, 0:1], float(BATCH * SEQ * HEADS * SETS) - 0.5,
                                                     None, ALU.is_lt), v_a)
        att.close()
        main_over = [bad_known, attn_done[TILES - 1], (p_a, p_a.value), (a_a, a_a.value), (g_a, g_a.value)]
        for q_ in (pe, act, dve, pool, sync):
            q_.wait(*main_over)
        general = general_attention(ctx, nc, dr, psum, main_over, stream, normed, attended, wqkv, wproj, eye)
        for q_, g_ in zip((pe, act, dve, pool, sync), general):
            q_.branch(bad, g_)

        def store(ch, acc):
            sync.wait(acc)
            t0 = ch * FFN_TILES
            sync.dma(lambda e: e.dma_start(out_tiles[:, t0:t0 + FFN_TILES, :], attended[:, t0:t0 + FFN_TILES, :]), s_out)

        moe("second", attended, lambda t: None, store, None, [])
        sync.wait((s_out, s_out.value))

        block = ctx.enter_context(nc.Block())
        block.sync(lambda e: sync.play(e))
        block.gpsimd(lambda e: pool.play(e))
        block.scalar(lambda e: act.play(e))
        block.vector(lambda e: dve.play(e))
        block.tensor(lambda e: pe.play(e))


OUT_SHAPE = (BATCH, SEQ, D)


def kernel(**inputs):
    import concourse.bacc as bacc
    from concourse.bass_utils import run_bass_kernel_spmd

    arrays = {k: np.ascontiguousarray(v) for k, v in inputs.items()
              if k not in ("L0_attn_b_W_attn", "L0_attn_b_W_proj", "L0_ffn_b1", "L0_attn_a_C_im")}
    arrays["w_attn_cols"] = np.ascontiguousarray(np.asarray(inputs["L0_attn_b_W_attn"]).T)
    arrays["w_proj_rows"] = np.ascontiguousarray(
        np.asarray(inputs["L0_attn_b_W_proj"]).T.reshape(SETS, P, D).transpose(1, 0, 2))
    arrays["b1_cols"] = np.ascontiguousarray(np.asarray(inputs["L0_ffn_b1"]).reshape(EXPERTS * HBLK, P).T)
    arrays.update(shape_constants())
    nc = bacc.Bacc("TRN2", target_bir_lowering=False, num_devices=1)
    dr = {k: nc.dram_tensor(k, a.shape, mybir.dt.from_np(a.dtype), kind="ExternalInput").ap()
          for k, a in arrays.items()}
    out = nc.dram_tensor("out", OUT_SHAPE, F32, kind="ExternalOutput").ap()
    build(nc, dr, out)
    r = run_bass_kernel_spmd(nc, [arrays], core_ids=[0])
    return r.results[0]["out"]
```

```python
import itertools
import math
from contextlib import ExitStack

import numpy as np

import concourse.bass as bass
from concourse import mybir

F32 = mybir.dt.float32
F16 = mybir.dt.float16
U32 = mybir.dt.uint32
ALU = mybir.AluOpType
ACT = mybir.ActivationFunctionType
AX_X = mybir.AxisListType.X

P = 128
BATCH, SEQ, D = 16, 256, 128
HALVES = SEQ // P
TILES = BATCH * HALVES
STATES = 64
EXPERTS, HIDDEN = 8, 256
HBLK = HIDDEN // P
HEADS, SETS = 16, 4
HD = D // HEADS
EPS = 1e-5
FREQ = 2 * SEQ
BANK = 512

CONV_BATCHES = 4
CONV_CHUNKS = BATCH // CONV_BATCHES
FFN_TILES = 4
FFN_CHUNKS = TILES // FFN_TILES

QUADS, LANES = 4, 4
SLOT = 32
SCALE = 1.0 / math.sqrt(HD)
PAIRS = SETS // 2
UNIT = 3 * 2 * P

RDEN_MIN, RDEN_MAX = 1e-15, 1e25
MASKED = -1e38

WSCALE = 64.0
W_MIN, W_MAX, B1_MAX = 2.0 ** -3, 2.0 ** 7, 2.0 ** 13


def dft_constants():
    n = np.arange(SEQ)
    f = np.arange(SEQ)
    ang = 2.0 * np.pi * np.outer(f, n) / FREQ
    cos, sin = np.cos(ang), -np.sin(ang)
    nyq = np.cos(np.pi * n)
    sin_packed = sin.copy()
    sin_packed[0] = nyq
    forward = np.concatenate([cos, sin_packed])
    cos_last = cos[:P].copy()
    cos_last[0] = nyq
    taps = np.concatenate([cos, sin, cos_last])
    weight = np.full((SEQ, 1), 2.0 / FREQ)
    weight[0] = 1.0 / FREQ
    inverse = np.concatenate([weight * cos, np.concatenate([nyq[None] / FREQ, (weight * sin)[1:]])])

    def by_sample(m):
        return np.ascontiguousarray(m.T.reshape(HALVES, P, m.shape[0]).transpose(1, 0, 2)).astype(np.float32)

    inv = np.ascontiguousarray(inverse.reshape(4, P, SEQ).transpose(1, 0, 2)).astype(np.float32)
    return by_sample(forward), by_sample(taps), inv


def shape_constants():
    forward, taps, inverse = dft_constants()
    k = np.arange(P)[:, None]
    q = np.arange(P)[None, :]
    keep = np.where(k <= q, 1.0, 0.0).astype(np.float32)
    return {
        "c_forward": forward,
        "c_taps": taps,
        "c_inverse": inverse,
        "c_ramp": np.tile(np.arange(SEQ, dtype=np.float32), (P, 1)),
        "c_eye": np.eye(P, dtype=np.float32),
        "c_keep": np.concatenate([keep, keep], axis=1),
        "c_masked": np.stack([np.where(np.arange(SEQ)[None, :] <= k + P * h, 0.0, MASKED) for h in range(HALVES)],
                             axis=1).astype(np.float32),
        "c_lanes": (np.arange(P)[:, None] // HD % LANES == np.arange(LANES)[None, :]).astype(np.float32),
        "c_expert": np.tile(np.arange(EXPERTS, dtype=np.float32), (P, FFN_TILES, 1)),
    }


class Signal:

    def __init__(self, ctx, nc, name):
        self.sem, self.value = ctx.enter_context(nc.semaphore(name)), 0

    def add(self, n):
        self.value += n
        return (self, self.value)


class Stream:

    def __init__(self, name):
        self.name, self.items, self.seen = name, [], {}

    def wait(self, *events):
        for ev in events:
            if ev is None:
                continue
            signal, value = ev
            if self.seen.get(signal, 0) < value:
                self.seen[signal] = value
                self.items.append((signal.sem, value))

    def do(self, build, signal=None):
        self.items.append((build, signal.sem if signal else None, 1))
        return signal.add(1) if signal else None

    def dma(self, build, signal):
        self.items.append((build, signal.sem, 16))
        return signal.add(16)

    def branch(self, flag, body):
        def build(e):
            with e.If(e.value_load(flag[0:1, 0:1], min_val=0, max_val=1)):
                body(e)
        self.items.append((build, None, 1))

    def play(self, eng):
        for item in self.items:
            if len(item) == 2:
                eng.wait_ge(*item)
            else:
                ins = item[0](eng)
                if item[1] is not None:
                    ins.then_inc(item[1], item[2])


class Crew:

    def __init__(self, ctx, nc, tag):
        self.streams = [Stream(n) for n in ("tensor", "scalar", "vector", "gpsimd", "sync")]
        self.pe, self.act, self.dve, self.pool, self.sync = self.streams
        self.signals = [Signal(ctx, nc, f"{n}_{tag}") for n in ("tensor", "scalar", "vector", "gpsimd")]
        self.stored = Signal(ctx, nc, f"stored_{tag}")

    def issued(self):
        return [(sg, sg.value) for sg in (*self.signals, self.stored) if sg.value]


class Banks:

    def __init__(self, psum, numbers):
        self.views = [psum[:, n * BANK:(n + 1) * BANK] for n in numbers]
        self.free, self.at = [[] for _ in numbers], 0

    def take(self):
        i = self.at
        self.at = (i + 1) % len(self.views)
        before, self.free[i] = self.free[i], []
        return self.views[i], before, self.free[i]


def general_attention(ctx, nc, dr, psum, start, stream, normed, attended, wqkv, wproj, eye):
    own = ExitStack()

    def sb(name, shape, dt=F32):
        return own.enter_context(nc.sbuf_tensor(name, shape, dt))

    BH = BATCH * HEADS
    xt = sb("gen_xt", [P, SEQ])
    qk = sb("gen_qk", [P, SETS + 1, SEQ])
    vt = sb("gen_v", [P, HALVES, D])
    q_h, k_h = sb("gen_q_head", [HD, SETS, SEQ]), sb("gen_k_head", [HD, SEQ])
    v_h = sb("gen_v_head", [P, HALVES, HD])
    masked = sb("gen_masked", [P, HALVES, SEQ])
    raw = sb("gen_scores", [P, SETS, HALVES, SEQ])
    peak, shift = sb("gen_peak", [P, SETS * HALVES]), sb("gen_shift", [P, SETS * HALVES])
    weights = sb("gen_weights", [P, SETS * HALVES, SEQ])
    total, inv = sb("gen_total", [P, SETS * HALVES]), sb("gen_inverse", [P, SETS * HALVES])
    turned_w = sb("gen_turned", [P, SETS, 4 * P])
    o_h = sb("gen_out", [P, SETS * HALVES, HD])
    o_tok, o_rows = sb("gen_out_tokens", [P, SETS * D]), sb("gen_out_rows", [P, SETS * P])
    dq = nc.dram_tensor("gen_q", [BH, SETS, HD, SEQ], F32, kind="Internal").ap()
    dk = nc.dram_tensor("gen_k", [BH, HD, SEQ], F32, kind="Internal").ap()
    dv = nc.dram_tensor("gen_v_rows", [BH, SEQ, HD], F32, kind="Internal").ap()
    do = nc.dram_tensor("gen_o", [BH, SETS, SEQ, HD], F32, kind="Internal").ap()
    own.close()

    def sig(name):
        return Signal(ctx, nc, name)

    pe, act, dve, sync = (Stream(n) for n in ("tensor", "scalar", "vector", "sync"))
    p_g, a_g, v_g, s_g = sig("tensor_general"), sig("scalar_general"), sig("vector_general"), sig("landed_general")
    for q in (pe, act, dve, sync):
        q.wait(*start)
    mask_here = sync.dma(lambda e: e.dma_start(masked[:], dr["c_masked"]), s_g)

    wrote = None
    for b in range(BATCH):
        heads = slice(b * HEADS, (b + 1) * HEADS)
        pe.wait(wrote)
        for h in range(HALVES):
            done = pe.do(lambda e, h=h, b=b: e.transpose(psum[:, h * P:(h + 1) * P], normed[:, HALVES * b + h, :],
                                                         eye[:]), p_g)
        act.wait(done)
        done = act.do(lambda e: e.copy(xt[:], psum[:, 0:SEQ]), a_g)
        pe.wait(done)
        for g in range(SETS + 1):
            done = pe.do(lambda e, g=g: e.matmul(psum[:, (g + 1) * BANK:(g + 1) * BANK + SEQ],
                                                 wqkv[:, g * D:(g + 1) * D], xt[:], start=True, stop=True), p_g)
        for h in range(HALVES):
            done = pe.do(lambda e, h=h: e.matmul(psum[:, (6 + h) * BANK:(6 + h) * BANK + D],
                                                 xt[:, h * P:(h + 1) * P], wqkv[:, (SETS + 1) * D:(SETS + 2) * D],
                                                 start=True, stop=True), p_g)
        act.wait(done)
        for g in range(SETS + 1):
            act.do(lambda e, g=g: e.copy(qk[:, g, :], psum[:, (g + 1) * BANK:(g + 1) * BANK + SEQ]), a_g)
        for h in range(HALVES):
            done = act.do(lambda e, h=h: e.copy(vt[:, h, :], psum[:, (6 + h) * BANK:(6 + h) * BANK + D]), a_g)
        sync.wait(done)
        for g in range(SETS):
            sync.dma(lambda e, g=g, heads=heads: e.dma_start(dq[heads, g], qk[:, g, :]), s_g)
        sync.dma(lambda e, heads=heads: e.dma_start(dk[heads], qk[:, SETS, :]), s_g)
        for h in range(HALVES):
            wrote = sync.dma(lambda e, h=h, heads=heads: e.dma_start(
                dv[heads, h * P:(h + 1) * P, :].rearrange("n t d -> t n d"),
                vt[:, h, :].rearrange("t (n d) -> t n d", d=HD)), s_g)
    pe.wait(wrote)
    act.wait(wrote)
    dve.wait(wrote, mask_here)
    sync.wait(wrote)

    l_in, l_p, l_v, l_a, l_out = (sig(n) for n in ("loop_loads", "loop_tensor", "loop_vector", "loop_scalar",
                                                   "loop_stores"))
    IN, PEN, VN, AN, OUTN = 16 * (2 + HALVES), 3, 5, 2, 16 * SETS

    def loop_sync(e):
        e.sem_inc(l_out.sem, 1)
        with e.Fori(0, BH) as i:
            e.wait_ge(l_out.sem, i * OUTN + 1)
            e.dma_start(q_h[:], dq[bass.ds(i, 1)].rearrange("a g d t -> d (a g) t")).then_inc(l_in.sem, 16)
            e.dma_start(k_h[:], dk[bass.ds(i, 1)].rearrange("a d t -> d (a t)")).then_inc(l_in.sem, 16)
            for h in range(HALVES):
                e.dma_start(v_h[:, h, :], dv[bass.ds(i, 1), h * P:(h + 1) * P].rearrange("a t d -> t (a d)"))\
                 .then_inc(l_in.sem, 16)
            e.wait_ge(l_v.sem, i * VN + VN)
            for g in range(SETS):
                e.dma_start(do[bass.ds(i, 1), g].rearrange("a (h t) d -> t (a h) d", h=HALVES),
                            o_h[:, g * HALVES:(g + 1) * HALVES, :]).then_inc(l_out.sem, 16)

    def loop_pe(e):
        with e.Fori(0, BH) as i:
            e.wait_ge(l_in.sem, i * IN + IN)
            for g in range(SETS):
                for h in range(HALVES):
                    last = e.matmul(psum[:, g * BANK + h * SEQ:g * BANK + (h + 1) * SEQ], q_h[:, g, h * P:(h + 1) * P],
                                    k_h[:], start=True, stop=True)
            last.then_inc(l_p.sem, 1)
            e.wait_ge(l_v.sem, i * VN + 4)
            for g in range(SETS):
                for k in range(HALVES):
                    for h in range(HALVES):
                        at = (SETS + g) * BANK + (k * HALVES + h) * P
                        last = e.transpose(psum[:, at:at + P], weights[:, g * HALVES + h, k * P:(k + 1) * P], eye[:])
            last.then_inc(l_p.sem, 1)
            e.wait_ge(l_a.sem, i * AN + 2)
            for g in range(SETS):
                for h in range(HALVES):
                    for k in range(HALVES):
                        at = (k * HALVES + h) * P
                        last = e.matmul(psum[:, (g * HALVES + h) * HD:(g * HALVES + h + 1) * HD],
                                        turned_w[:, g, at:at + P], v_h[:, k, :], start=(k == 0), stop=(k == HALVES - 1))
            last.then_inc(l_p.sem, 1)

    def loop_dve(e):
        with e.Fori(0, BH) as i:
            e.wait_ge(l_p.sem, i * PEN + 1)
            for g in range(SETS):
                last = e.tensor_tensor(raw[:, g], psum[:, g * BANK:g * BANK + HALVES * SEQ].rearrange(
                    "p (h k) -> p h k", k=SEQ), masked[:], ALU.add)
            last.then_inc(l_v.sem, 1)
            e.wait_ge(l_v.sem, i * VN + 1)
            e.reduce_max(peak[:], raw[:].rearrange("p g h k -> p (g h) k"), AX_X).then_inc(l_v.sem, 1)
            e.wait_ge(l_v.sem, i * VN + 2)
            e.tensor_scalar(shift[:], peak[:], -SCALE, None, ALU.mult).then_inc(l_v.sem, 1)
            e.wait_ge(l_a.sem, i * AN + 1)
            e.reciprocal(inv[:], total[:]).then_inc(l_t.sem, 1)
            e.wait_ge(l_t.sem, i + 1)
            e.tensor_tensor(weights[:], weights[:], inv[:].rearrange("p (n a) -> p n a", a=1).to_broadcast(
                [P, SETS * HALVES, SEQ]), ALU.mult).then_inc(l_v.sem, 1)
            e.wait_ge(l_p.sem, i * PEN + 3)
            e.tensor_copy(o_h[:], psum[:, 0:SETS * HALVES * HD].rearrange("p (n d) -> p n d", d=HD))\
             .then_inc(l_v.sem, 1)

    l_t = sig("loop_inverse")

    def loop_act(e):
        with e.Fori(0, BH) as i:
            e.wait_ge(l_v.sem, i * VN + 3)
            for n in range(SETS * HALVES):
                last = e.activation(weights[:, n, :], raw[:, n // HALVES, n % HALVES, :], ACT.Exp, scale=SCALE,
                                    bias=shift[:, n:n + 1], accum_out=total[:, n:n + 1])
            last.then_inc(l_a.sem, 1)
            e.wait_ge(l_p.sem, i * PEN + 2)
            e.copy(turned_w[:].rearrange("p g n -> p (g n)"), psum[:, SETS * BANK:2 * SETS * BANK]).then_inc(l_a.sem, 1)

    tails = [Stream(n) for n in ("tensor", "scalar", "vector", "sync")]
    tpe, tact, tdve, tsync = tails
    stored = (l_out, BH * OUTN + 1)
    tsync.wait(stored)
    tpe.wait(stored)
    added = None
    for t in range(TILES):
        b, h = divmod(t, HALVES)
        tsync.wait(added)
        for n in range(HEADS):
            got = tsync.dma(lambda e, n=n, b=b, h=h: e.dma_start(
                o_tok[:].rearrange("p (g l c d) -> p g l c d", g=SETS, l=LANES, d=HD)[:, :, n % LANES, n // LANES, :],
                do[b * HEADS + n, :, h * P:(h + 1) * P, :].rearrange("g t d -> t g d")), s_g)
        tpe.wait(got)
        for g in range(SETS):
            done = tpe.do(lambda e, g=g: e.transpose(psum[:, g * P:(g + 1) * P], o_tok[:, g * D:(g + 1) * D], eye[:]), p_g)
        tact.wait(done)
        done = tact.do(lambda e: e.copy(o_rows[:], psum[:, 0:SETS * P]), a_g)
        tpe.wait(done)
        for g in range(SETS):
            done = tpe.do(lambda e, g=g: e.matmul(psum[:, BANK:BANK + D], o_rows[:, g * P:(g + 1) * P], wproj[:, g, :],
                                                  start=(g == 0), stop=(g == SETS - 1)), p_g)
        tdve.wait(done)
        added = tdve.do(lambda e, t=t: e.tensor_tensor(attended[:, t, :], psum[:, BANK:BANK + D], stream[:, t, :],
                                                       ALU.add), v_g)
    bodies = []
    for head, loop, tail in ((pe, loop_pe, tpe), (act, loop_act, tact), (dve, loop_dve, tdve),
                             (None, None, None), (sync, loop_sync, tsync)):
        def body(e, head=head, loop=loop, tail=tail):
            if head is not None:
                head.play(e)
                loop(e)
                tail.play(e)
            e.wait_ge(added[0].sem, added[1])
        bodies.append(body)
    return bodies


def front_buffers(nc, ctx, tag):
    def sb(name, shape, dt=F32):
        return ctx.enter_context(nc.sbuf_tensor(name + tag, shape, dt))

    CH = FFN_TILES * P
    return {
        "xt": sb("xt", [P, 2, CH]), "xt_parts": sb("xt_parts", [P, 2, 2, CH], F16),
        "logits": sb("logits", [P, 2, FFN_TILES, EXPERTS]), "top": sb("top", [P, 2, FFN_TILES, 8]),
        "top_at": sb("top_at", [P, 2, FFN_TILES, 8], U32), "top_no": sb("top_no", [P, 2, FFN_TILES, 2]),
        "gap": sb("gap", [P, 2, FFN_TILES]), "wpair": sb("wpair", [P, 2, 2, FFN_TILES]),
        "pick": sb("pick", [P, 2, 2, FFN_TILES, EXPERTS]), "comb": sb("comb", [P, 2, FFN_TILES, EXPERTS]),
        "comb_y": sb("comb_y", [P, 2, FFN_TILES, EXPERTS]), "comb_t": sb("comb_t", [EXPERTS, 2, CH]),
    }


def build(nc, dr, out):
    with ExitStack() as ctx:
        def sb(name, shape, dt=F32):
            return ctx.enter_context(nc.sbuf_tensor(name, shape, dt))

        def sig(name):
            return Signal(ctx, nc, name)

        main_crew = Crew(ctx, nc, "experts")
        pe, act, dve, pool, sync = main_crew.streams
        psum = ctx.enter_context(nc.psum_tensor("psum", [P, 8 * BANK], F32))

        stream = sb("stream", [P, TILES, D])
        mixed = sb("mixed", [P, TILES, D])
        good = sb("good", [P, BATCH + 1])
        bad = sb("bad", [1, 1], mybir.dt.int32)
        bad_weights, bad_scores = sb("bad_weights", [1, 1]), sb("bad_scores", [1, 1])
        widest = sb("widest", [P, 2 * EXPERTS])
        extent = sb("extent", [P, 4])
        extents = sb("extents", [1, 4])
        within = sb("within", [1, 4])
        normed = sb("normed", [P, TILES, D])
        stats = sb("stats", [P, TILES, 6])
        meanvar = sb("meanvar", [P, TILES, 2])
        rstd = sb("rstd", [P, TILES])
        vareps = sb("vareps", [P, TILES])
        minus_half = sb("minus_half", [P, TILES])
        eye = sb("eye", [P, P])
        ramp = sb("ramp", [P, SEQ])
        keep = sb("keep", [P, 2 * P])
        lanes = sb("lanes", [P, LANES])
        expert_no = sb("expert_no", [P, FFN_TILES, EXPERTS])
        wg = sb("wg", [P, EXPERTS])
        bg = sb("bg", [P, EXPERTS])
        w1 = sb("w1_parts", [P, 2, EXPERTS, HIDDEN], F16)
        b1 = sb("b1", [P, EXPERTS * HBLK])
        w2 = sb("w2_parts", [P, 2, EXPERTS * HBLK, D], F16)
        b2 = sb("b2", [EXPERTS, D])
        wqkv = sb("wqkv", [P, (SETS + 2) * D])
        wqkv_parts = sb("wqkv_parts", [P, 2, SETS + 2, D], F16)
        wproj = sb("wproj", [P, SETS, D])

        s_small, s_forward, s_dft, s_w1, s_w2, s_expw, s_attw, s_kept = (sig(n) for n in (
            "landed_small", "landed_forward", "landed_dft", "landed_w1", "landed_w2", "landed_expert_rows",
            "landed_attn_weights", "kept_x"))
        s_x = [sig(f"landed_x{i}") for i in range(CONV_CHUNKS)]
        v_ln, g_ln = sig("vector_ln"), sig("gpsimd_ln")
        v_w, p_w = sig("vector_weight_range"), sig("tensor_weight_range")

        def load(dst, src, signal):
            return sync.dma(lambda e: e.dma_start(dst, src), signal)

        x_tiles = dr["L0_attn_a_u"].rearrange("b (h p) m -> p (b h) m", p=P)
        out_tiles = out.rearrange("b (h p) m -> p (b h) m", p=P)
        front = front_buffers(nc, ctx, "")
        conv_ctx = ExitStack()

        def csb(name, shape, dt=F32):
            return conv_ctx.enter_context(nc.sbuf_tensor(name, shape, dt))

        a_log, c_re = csb("a_log", [P, STATES]), csb("c_re", [P, STATES])
        log_dt, skip_d = csb("log_dt", [P, 1]), csb("skip_d", [P, 1])
        forward = csb("forward", [P, HALVES, 4 * P])
        taps = csb("taps", [P, HALVES, 5 * P])
        inverse = csb("inverse", [P, 4, SEQ])
        w1_whole = csb("w1_whole", [P, EXPERTS, HIDDEN])
        w2_whole = csb("w2_whole", [P, EXPERTS * HBLK, D])
        w1_rows = dr["L0_ffn_W1"].rearrange("e d h -> d e h")
        w2_rows = dr["L0_ffn_W2"].rearrange("e (k p) d -> p (e k) d", p=P)
        tiles_per = CONV_BATCHES * HALVES

        def load_x(i):
            tiles = slice(i * tiles_per, (i + 1) * tiles_per)
            return load(stream[:, tiles, :], x_tiles[:, tiles, :], s_x[i])

        load(a_log[:], dr["L0_attn_a_A_log"].rearrange("(a n) -> a n", a=1).to_broadcast([P, STATES]), s_small)
        load(log_dt[:], dr["L0_attn_a_log_dt"].rearrange("(p a) -> p a", a=1), s_small)
        load(ramp[:], dr["c_ramp"], s_small)
        load(c_re[:], dr["L0_attn_a_C_re"], s_small)
        load(eye[:], dr["c_eye"], s_small)
        small_here = load(skip_d[:], dr["L0_attn_a_D"].rearrange("(p a) -> p a", a=1), s_small)
        x_here = [load_x(0)]
        forward_here = load(forward[:], dr["c_forward"], s_forward)
        w1_here = load(w1_whole[:], w1_rows, s_w1)
        x_here.append(load_x(1))
        w2_here = load(w2_whole[:], w2_rows, s_w2)
        load(taps[:], dr["c_taps"], s_dft)
        dft_here = load(inverse[:], dr["c_inverse"], s_dft)
        x_here += [load_x(2), load_x(3)]
        load(wg[:], dr["L0_ffn_Wg"], s_expw)
        load(bg[:], dr["L0_ffn_bg"].rearrange("(a n) -> a n", a=1).to_broadcast([P, EXPERTS]), s_expw)
        load(expert_no[:], dr["c_expert"], s_expw)
        load(b1[:], dr["b1_cols"], s_expw)
        expw_here = load(b2[:], dr["L0_ffn_b2"], s_expw)
        load(keep[:], dr["c_keep"], s_attw)
        load(lanes[:], dr["c_lanes"], s_attw)
        load(wqkv[:], dr["w_attn_cols"], s_attw)
        attw_here = load(wproj[:], dr["w_proj_rows"], s_attw)

        pow_ready = pool.do(lambda e: e.memset(minus_half[:], -0.5), g_ln)

        def layer_norm(x, t0, n, ready, dve=dve, pool=pool, v_ln=v_ln, g_ln=g_ln):
            dve.wait(*ready)
            for t in range(t0, t0 + n):
                stats_done = dve.do(lambda e, t=t: e.bn_stats(stats[:, t, :], x[:, t, :]), v_ln)
            dve.wait(stats_done)
            for t in range(t0, t0 + n):
                agg = dve.do(lambda e, t=t: e.bn_aggr(meanvar[:, t, :], stats[:, t, :]), v_ln)
            pool.wait(agg, pow_ready)
            eps_done = pool.do(lambda e: e.tensor_scalar(vareps[:, t0:t0 + n], meanvar[:, t0:t0 + n, 1], EPS, None,
                                                         ALU.add), g_ln)
            pool.wait(eps_done)
            rstd_done = pool.do(lambda e: e.tensor_tensor(rstd[:, t0:t0 + n], vareps[:, t0:t0 + n],
                                                          minus_half[:, t0:t0 + n], ALU.pow), g_ln)
            yield
            dve.wait(rstd_done)
            for t in range(t0, t0 + n):
                done = dve.do(lambda e, t=t: e.tensor_scalar(normed[:, t, :], x[:, t, :], meanvar[:, t, 0:1],
                                                             rstd[:, t:t + 1], ALU.subtract, ALU.mult), v_ln)
            yield done

        def spaced(gen):
            for _ in gen:
                yield
                yield

        def last(gen):
            got = None
            for got in gen:
                pass
            return got

        a_k, v_k, p_k, g_k = sig("scalar_taps"), sig("vector_taps"), sig("tensor_taps"), sig("gpsimd_weights")
        v_y, g_y, p_f, p_y = sig("vector_conv"), sig("gpsimd_conv"), sig("tensor_forward"), sig("tensor_inverse")
        CHAINS, ERING, ON_VECTOR = 2, 8, (1, 3, 5, 7)
        neg_a, dt, z = csb("neg_a", [P, STATES]), csb("dt", [P, 1]), csb("z", [P, STATES])
        decay = csb("decay", [P, ERING, SEQ])
        chain = csb("chain", [P, CHAINS, SEQ])
        spread = csb("spread", [P, ERING, P])
        ktap = csb("ktap", [P, HALVES, D])
        khat = csb("khat", [P, 5, D])
        wide, narrow, misc = Banks(psum, [0, 1, 2, 3]), Banks(psum, [4, 5]), Banks(psum, [6, 7])
        norms = [layer_norm(stream, ch * tiles_per, tiles_per, [x_here[ch]]) for ch in range(CONV_CHUNKS)]
        ln_ready = {}

        scaled_weights, weight_cuts = [], []

        def scale_weights(whole, parts, here):
            flat = whole[:].rearrange("p e h -> p (e h)")
            pool.wait(here)
            scaled_weights.append((flat, parts, pool.do(
                lambda e: e.tensor_scalar(flat, flat, WSCALE, None, ALU.mult), g_k)))

        def cut_weights():
            flat = mixed[:, TILES - (SETS + 2):TILES, :].rearrange("p t m -> p (t m)")
            act.wait(attw_here)
            scaled_weights.append((flat, wqkv_parts, act.do(lambda e: e.mul(flat, wqkv[:], WSCALE), a_k)))
            for flat, parts, scaled in scaled_weights:
                high = parts[:, 0].rearrange("p e h -> p (e h)")
                act.wait(scaled)
                weight_cuts.append((flat, parts, act.do(lambda e, flat=flat, high=high: e.copy(high, flat), a_k)))

        def low_weights(n, of):
            for flat, parts, high_done in weight_cuts:
                high, low = (parts[:, k].rearrange("p e h -> p (e h)") for k in range(2))
                share = flat.shape[1] // of
                cols = slice(n * share, (n + 1) * share)
                pool.wait(high_done)
                done = pool.do(lambda e, flat=flat, high=high, low=low, cols=cols: e.tensor_tensor(
                    low[:, cols], flat[:, cols], high[:, cols], ALU.subtract), g_k)
            return done

        act.wait(small_here)
        act.do(lambda e: e.activation(neg_a[:], a_log[:], ACT.Exp), a_k)
        exps_done = act.do(lambda e: e.activation(dt[:], log_dt[:], ACT.Exp), a_k)
        dve.wait(exps_done)
        z_done = dve.do(lambda e: e.tensor_scalar(z[:], neg_a[:], dt[:, 0:1], -1.0, ALU.mult, ALU.mult), v_k)
        act.wait(z_done)
        dve.wait(small_here)
        prod = csb("prod", [P, 2, 4, BANK])
        yhat = csb("yhat", [P, 2, 4, BANK])
        conv_done = []
        yhat_read, prod_read = [None, None], [None, None]
        fwd, y_done, inv_done = {}, {}, {}

        FORWARD_ORDER = (0, 2, 1, 3)

        def forward_chunk(ch, blocks=FORWARD_ORDER):
            un = normed[:, ch * tiles_per:(ch + 1) * tiles_per, :].rearrange("p (b h) m -> p h b m", h=HALVES)
            pe.wait(ln_ready[ch])
            for i in blocks:
                bank, before, free = wide.take()
                pe.wait(*before)
                for h in range(HALVES):
                    done = pe.do(lambda e, i=i, h=h, bank=bank, un=un: e.matmul(
                        bank, forward[:, h, i * P:(i + 1) * P], un[:, h], start=(h == 0), stop=(h == HALVES - 1)),
                        p_f if h == HALVES - 1 else None)
                fwd[ch, i] = (bank, free, done)

        def products(ch):
            s = ch % 2
            y_done[ch] = []
            for f in range(2):
                (re, re_free, re_done), (im, im_free, im_done) = fwd[ch, f], fwd[ch, 2 + f]
                dve.wait(re_done, im_done, prod_read[f])
                last_cos = 4 if f == 0 else 1
                for n, (src, free, k) in enumerate(((re, re_free, f), (im, im_free, 2 + f),
                                                    (re, re_free, 2 + f), (im, im_free, last_cos))):
                    done = dve.do(lambda e, n=n, src=src, k=k, f=f: e.tensor_tensor(
                        prod[:, f, n, :].rearrange("p (b m) -> p b m", m=D), src.rearrange("p (b m) -> p b m", m=D),
                        khat[:, k:k + 1, :].to_broadcast([P, CONV_BATCHES, D]), ALU.mult), v_y)
                    if n >= 2:
                        free.append(done)
                    if n == 1:
                        both = done
                pool.wait(both, yhat_read[s])
                eng_re = pool.do(lambda e, s=s, f=f: e.tensor_tensor(yhat[:, s, f, :], prod[:, f, 0, :], prod[:, f, 1, :],
                                                                     ALU.subtract), g_y)
                pool.wait(done)
                eng_im = pool.do(lambda e, s=s, f=f: e.tensor_tensor(yhat[:, s, 2 + f, :], prod[:, f, 2, :],
                                                                     prod[:, f, 3, :], ALU.add), g_y)
                prod_read[f] = eng_im
                y_done[ch] += [eng_re, eng_im]

        def inverse_chunk(ch):
            s = ch % 2
            pe.wait(*y_done[ch])
            for h in range(HALVES):
                bank, before, free = narrow.take()
                pe.wait(*before)
                for i in range(4):
                    done = pe.do(lambda e, i=i, h=h, s=s, bank=bank: e.matmul(
                        bank, inverse[:, i, h * P:(h + 1) * P], yhat[:, s, i, :], start=(i == 0), stop=(i == 3)),
                        p_y if i == 3 else None)
                yhat_read[s] = done
                inv_done[ch, h] = (bank, free, done)

        def residual(ch):
            for h in range(HALVES):
                bank, free, done = inv_done[ch, h]
                dve.wait(done)
                half = stream[:, ch * tiles_per:(ch + 1) * tiles_per, :].rearrange("p (b h) m -> p h b m", h=HALVES)[:, h]
                added = dve.do(lambda e, bank=bank, half=half: e.tensor_tensor(
                    half, bank.rearrange("p (b m) -> p b m", m=D), half, ALU.add), v_y)
                free.append(added)
            conv_done.append(added)

        CH = FFN_TILES * P

        def moe(tag, crew, whole, rings, front, x, y, ready_of_tile, after_chunk, tick):
            pe, act, dve, pool, sync = crew.streams
            p_e, a_e, v_e, g_e = crew.signals
            HRING = 4
            xt, logits, top, top_at = (front[n] for n in ("xt", "logits", "top", "top_at"))
            top_no, gap, wpair, pick = (front[n] for n in ("top_no", "gap", "wpair", "pick"))
            comb, comb_y, comb_t, xt_parts = (front[n] for n in ("comb", "comb_y", "comb_t", "xt_parts"))
            scale = 1.0 if whole else WSCALE
            misc, hb, yb = rings
            xt_free, comb_free, combt_free, hid_free = [None] * 2, [None] * 2, [None] * 2, [None] * HRING
            state, hid = {}, {}

            def prologue(ch):
                s, t0 = ch % 2, ch * FFN_TILES
                gen = layer_norm(x, t0, FFN_TILES, [ready_of_tile(t) for t in range(t0, t0 + FFN_TILES)],
                                 dve, pool, v_e, g_e)
                next(gen)
                yield
                normed_done = last(gen)
                yield
                bank, before, free = misc.take()
                pe.wait(normed_done, *before)
                for i in range(FFN_TILES):
                    done = pe.do(lambda e, i=i, bank=bank: e.transpose(bank[:, i * P:(i + 1) * P], normed[:, t0 + i, :],
                                                                       eye[:]), p_e if i == FFN_TILES - 1 else None)
                act.wait(done, xt_free[s])
                xt_done = act.do(lambda e, bank=bank: e.copy(xt[:, s, :], bank), a_e)
                x_ready = [xt_done]
                if not whole:
                    x_high = act.do(lambda e, bank=bank: e.copy(xt_parts[:, s, 0, :], bank), a_e)
                    free.append(x_high)
                    pool.wait(x_high)
                    x_low = pool.do(lambda e: e.tensor_tensor(xt_parts[:, s, 1, :], xt[:, s, :], xt_parts[:, s, 0, :],
                                                              ALU.subtract), g_e)
                    x_ready = [x_high, x_low]
                free.append(xt_done)
                state[ch, "x"] = x_ready
                yield
                bank, before, free = misc.take()
                pe.wait(xt_done, *before)
                for i in range(FFN_TILES):
                    done = pe.do(lambda e, i=i, bank=bank: e.matmul(bank[:, i * EXPERTS:(i + 1) * EXPERTS],
                                                                    xt[:, s, i * P:(i + 1) * P], wg[:],
                                                                    start=True, stop=True),
                                 p_e if i == FFN_TILES - 1 else None)
                dve.wait(done)
                lg = logits[:, s]
                lg_done = dve.do(lambda e, bank=bank: e.tensor_tensor(
                    lg, bank[:, 0:FFN_TILES * EXPERTS].rearrange("p (t e) -> p t e", e=EXPERTS),
                    bg[:].rearrange("p (a e) -> p a e", a=1).to_broadcast([P, FFN_TILES, EXPERTS]), ALU.add), v_e)
                free.append(lg_done)
                dve.wait(lg_done)
                for i in range(FFN_TILES):
                    tops = dve.do(lambda e, i=i: e.max(top[:, s, i, :], logits[:, s, i, :]), v_e)
                dve.wait(tops)
                for i in range(FFN_TILES):
                    found = dve.do(lambda e, i=i: e.max_index(top_at[:, s, i, :], top[:, s, i, :], logits[:, s, i, :]),
                                   v_e)
                gap_done = dve.do(lambda e: e.tensor_tensor(gap[:, s, :], top[:, s, :, 1], top[:, s, :, 0],
                                                            ALU.subtract), v_e)
                act.wait(gap_done)
                ex_done = act.do(lambda e: e.activation(gap[:, s, :], gap[:, s, :], ACT.Exp), a_e)
                yield
                dve.wait(found)
                no_done = dve.do(lambda e: e.tensor_copy(top_no[:, s], top_at[:, s, :, 0:2]), v_e)
                dve.wait(ex_done)
                den = dve.do(lambda e: e.tensor_scalar(wpair[:, s, 1, :], gap[:, s, :], 1.0, None, ALU.add), v_e)
                dve.wait(den)
                w0 = dve.do(lambda e: e.reciprocal(wpair[:, s, 0, :], wpair[:, s, 1, :]), v_e)
                dve.wait(no_done, w0)
                w1_ = dve.do(lambda e: e.tensor_tensor(wpair[:, s, 1, :], wpair[:, s, 0, :], gap[:, s, :], ALU.mult), v_e)
                for k in range(2):
                    picked = dve.do(lambda e, k=k: e.tensor_tensor(
                        pick[:, s, k], expert_no[:], top_no[:, s, :, k:k + 1].to_broadcast([P, FFN_TILES, EXPERTS]),
                        ALU.is_equal), v_e)
                dve.wait(w1_, picked)
                for k in range(2):
                    scaled = dve.do(lambda e, k=k: e.tensor_tensor(
                        pick[:, s, k], pick[:, s, k],
                        wpair[:, s, k, :].rearrange("p (t a) -> p t a", a=1).to_broadcast([P, FFN_TILES, EXPERTS]),
                        ALU.mult), v_e)
                dve.wait(scaled, comb_free[s])
                comb_done = dve.do(lambda e: e.tensor_tensor(comb[:, s], pick[:, s, 0], pick[:, s, 1], ALU.add), v_e)
                dve.wait(comb_done)
                comb_y_done = dve.do(lambda e: e.tensor_scalar(comb_y[:, s], comb[:, s], 1.0 / scale, None, ALU.mult),
                                     v_e)
                yield
                yield
                bank, before, free = misc.take()
                pe.wait(comb_done, *before)
                for i in range(FFN_TILES):
                    done = pe.do(lambda e, i=i, bank=bank: e.transpose(bank[0:EXPERTS, i * P:(i + 1) * P],
                                                                       comb[:, s, i, :], eye[:]),
                                 p_e if i == FFN_TILES - 1 else None)
                act.wait(done, combt_free[s])
                ct_done = act.do(lambda e, bank=bank: e.copy(comb_t[:, s, :], bank[0:EXPERTS, :]), a_e)
                free.append(ct_done)
                yield
                bank, before, free = misc.take()
                pe.wait(ct_done, *before)
                for i in range(FFN_TILES):
                    done = pe.do(lambda e, i=i, bank=bank: e.matmul(bank[:, i * P:(i + 1) * P],
                                                                    comb_t[:, s, i * P:(i + 1) * P], b2[:],
                                                                    start=True, stop=True),
                                 p_e if i == FFN_TILES - 1 else None)
                combt_free[s] = done
                dve.wait(done, comb_y_done)
                base = dve.do(lambda e, bank=bank: e.tensor_tensor(
                    y[:, t0:t0 + FFN_TILES, :], bank.rearrange("p (t m) -> p t m", m=D),
                    x[:, t0:t0 + FFN_TILES, :], ALU.add), v_e)
                free.append(base)
                state[ch, "base"] = base

            def up(ch, e_):
                s, r = ch % 2, (ch * EXPERTS + e_) % HRING
                there = []
                for k in range(HBLK):
                    bank, before, free = hb.take()
                    pe.wait(*state[ch, "x"], *before)
                    cols = slice(k * P, (k + 1) * P)
                    if whole:
                        done = pe.do(lambda e, cols=cols, bank=bank: e.matmul(bank, hid["w1"][:, e_, cols], xt[:, s, :],
                                                                              start=True, stop=True), p_e)
                    else:
                        for n, (w_part, x_part) in enumerate(PRODUCTS):
                            done = pe.do(lambda e, n=n, w_part=w_part, x_part=x_part, cols=cols, bank=bank: e.matmul(
                                bank, w1[:, w_part, e_, cols], xt_parts[:, s, x_part, :], start=(n == 0),
                                stop=(n == len(PRODUCTS) - 1)), p_e if n == len(PRODUCTS) - 1 else None)
                    act.wait(done, *(hid_free[r] or ()))

                    def relu(out, k=k, bank=bank):
                        return act.do(lambda e: e.activation(out, bank, ACT.Relu, scale=1.0 / scale,
                                                             bias=b1[:, e_ * HBLK + k:e_ * HBLK + k + 1]), a_e)
                    whole_done = relu(hid["whole"][:, r, k, :])
                    if whole:
                        there.append(whole_done)
                    else:
                        high = relu(hid["parts"][:, r, 0, k, :])
                        eng, sg = (dve, v_e) if k == 0 else (pool, g_e)
                        eng.wait(high)
                        there.append(high)
                        there.append(eng.do(lambda e, k=k: e.tensor_tensor(
                            hid["parts"][:, r, 1, k, :], hid["whole"][:, r, k, :], hid["parts"][:, r, 0, k, :],
                            ALU.subtract), sg))
                    free.append(whole_done if whole else high)
                if e_ == EXPERTS - 1:
                    xt_free[s] = done
                return there

            def down(ch, e_, there):
                s, r, t0 = ch % 2, (ch * EXPERTS + e_) % HRING, ch * FFN_TILES
                bank, before, free = yb.take()
                pe.wait(*there, *before)
                terms = ([(hid["whole"][:, r, k], hid["w2"][:, e_ * HBLK + k, :]) for k in range(HBLK)] if whole else
                         [(hid["parts"][:, r, h_part, k], w2[:, w_part, e_ * HBLK + k, :])
                          for k in range(HBLK) for h_part, w_part in PRODUCTS])
                for i in range(FFN_TILES):
                    for n, (h_, w_) in enumerate(terms):
                        done = pe.do(lambda e, i=i, n=n, h_=h_, w_=w_, bank=bank: e.matmul(
                            bank[:, i * P:(i + 1) * P], h_[:, i * P:(i + 1) * P], w_, start=(n == 0),
                            stop=(n == len(terms) - 1)),
                            p_e if i == FFN_TILES - 1 and n == len(terms) - 1 else None)
                hid_free[r] = (done, *there)
                dve.wait(done, state[ch, "base"], state.get((ch, "acc")))
                for i in range(FFN_TILES):
                    acc = dve.do(lambda e, i=i, bank=bank: e.scalar_tensor_tensor(
                        out=y[:, t0 + i, :], in0=bank[:, i * P:(i + 1) * P], scalar=comb_y[:, s, i, e_:e_ + 1],
                        in1=y[:, t0 + i, :], op0=ALU.mult, op1=ALU.add), v_e)
                free.append(acc)
                state[ch, "acc"] = acc
                if e_ == EXPERTS - 1:
                    comb_free[s] = acc
                    after_chunk(ch, acc)

            def run(first, buffers_free):
                own = ExitStack()

                def msb(name, shape, dt=F32):
                    return own.enter_context(nc.sbuf_tensor(f"{name}_{tag}", shape, dt))

                hid["whole"] = msb("hidden", [P, HRING, HBLK, CH])
                if whole:
                    hid["w1"], hid["w2"] = msb("w1", [P, EXPERTS, HIDDEN]), msb("w2", [P, EXPERTS * HBLK, D])
                    s_w = Signal(ctx, nc, f"landed_weights_{tag}")
                    sync.dma(lambda e: e.dma_start(hid["w1"][:], w1_rows), s_w)
                    pe.wait(sync.dma(lambda e: e.dma_start(hid["w2"][:], w2_rows), s_w))
                else:
                    hid["parts"] = msb("hidden_parts", [P, HRING, 2, HBLK, CH], F16)
                own.close()
                hid_free[:] = [tuple(buffers_free)] * HRING
                while (0, "x") not in state:
                    next(first)
                pending = []
                for ch in range(FFN_CHUNKS):
                    ahead = prologue(ch + 1) if ch + 1 < FFN_CHUNKS else iter(())
                    for e_ in range(EXPERTS):
                        pending.append((ch, e_, up(ch, e_)))
                        for _ in itertools.islice(first, 3):
                            pass
                        if len(pending) > LAG:
                            down(*pending.pop(0))
                        next(ahead, None)
                        tick(ch, e_)
                    for _ in ahead:
                        pass
                for p_ in pending:
                    down(*p_)
                return state[FFN_CHUNKS - 1, "acc"]

            return prologue(0), run

        def weight_range():
            for e_ in range(EXPERTS):
                for n, part in enumerate((w1[:, 0, e_, :], w2[:, 0, HBLK * e_:HBLK * (e_ + 1), :]
                                          .rearrange("p k d -> p (k d)"))):
                    at = n * EXPERTS + e_
                    found = dve.do(lambda e, part=part, at=at: e.tensor_reduce(
                        widest[:, at:at + 1], part, AX_X, ALU.max, apply_absolute_value=True), v_w)
                yield
            dve.wait(found)
            dve.do(lambda e: e.reduce_max(extent[:, 0:2], widest[:].rearrange("p (n e) -> p n e", n=2), AX_X), v_w)
            for at, part in ((2, wqkv_parts[:, 0].rearrange("p g d -> p (g d)")), (3, b1[:])):
                found = dve.do(lambda e, at=at, part=part: e.tensor_reduce(extent[:, at:at + 1], part, AX_X, ALU.max,
                                                                           apply_absolute_value=True), v_w)
            yield
            bank, before, free = misc.take()
            pe.wait(found, *before)
            for n in range(4):
                turned = pe.do(lambda e, n=n: e.transpose(bank[0:1, n * P:(n + 1) * P], extent[:, n:n + 1], eye[:]), p_w)
            dve.wait(turned)
            found = dve.do(lambda e: e.reduce_max(extents[:], bank[0:1, 0:4 * P].rearrange("a (n p) -> a n p", p=P), AX_X),
                           v_w)
            free.append(found)
            yield
            dve.wait(found)
            fits = dve.do(lambda e: e.tensor_scalar(within[:, 0:3], extents[:, 0:3], W_MIN * WSCALE, None, ALU.is_ge), v_w)
            dve.wait(fits)
            fits = dve.do(lambda e: e.scalar_tensor_tensor(out=within[:, 0:3], in0=extents[:, 0:3], scalar=W_MAX * WSCALE,
                                                           in1=within[:, 0:3], op0=ALU.is_le, op1=ALU.mult), v_w)
            fits = dve.do(lambda e: e.tensor_scalar(within[:, 3:4], extents[:, 3:4], B1_MAX, None, ALU.is_le), v_w)
            dve.wait(fits)
            fits = dve.do(lambda e: e.reduce_sum(extents[:, 0:1], within[:], AX_X), v_w)
            dve.wait(fits)
            dve.do(lambda e: e.tensor_scalar(bad_weights[:], extents[:, 0:1], 3.5, None, ALU.is_lt), v_w)
            yield

        PRODUCTS = ((0, 0), (0, 1), (1, 0))
        LAG = 2
        rings = (misc, wide, narrow)
        mixed_normed, norm_steps, range_steps = {}, {}, weight_range()

        def norm_mixed(ch, acc, crew, normed_at):
            for ev in layer_norm(mixed, ch * FFN_TILES, FFN_TILES, [acc], crew.dve, crew.pool, *crew.signals[2:]):
                normed_at[ch] = ev
                yield

        def tick_first(ch, e_):
            next(norm_steps.get(ch - 1, iter(())), None)
            if ch and e_ in (2, 5):
                next(range_steps, None)
            if (ch, e_) >= (FFN_CHUNKS - 2, 2):
                next(attn_first, None)

        first, run_first = moe("first", main_crew, False, rings, front, stream, mixed,
                               lambda t: conv_done[t // tiles_per],
                               lambda ch, acc: norm_steps.update({ch: norm_mixed(ch, acc, main_crew, mixed_normed)}),
                               tick_first)

        halves = [misc.take() for _ in range(HALVES)]
        LN_STEPS = {4: 0, 18: 0, 40: 1}
        scale_at = {18: (w1_whole, w1, w1_here), 22: (w2_whole, w2, w2_here)}
        FORWARD_AT = (26, 34, 42, 50)
        slot_read, spread_read, chain_sum = [None] * ERING, [None] * ERING, [None] * CHAINS
        opened, on_vector = [False], 0
        pe.wait(small_here)

        def add_taps(rows, columns, final=False):
            for h in range(HALVES):
                done = pe.do(lambda e, h=h, first=not opened[0]: e.matmul(
                    halves[h][0][:, 0:P], rows[:, h * P:(h + 1) * P], columns, start=first, stop=final),
                    p_k if h == HALVES - 1 else None)
            opened[0] = True
            return done

        for n in range(STATES):
            r = n % ERING
            act.wait(slot_read[r])
            decayed = act.do(lambda e, n=n, r=r: e.activation(decay[:, r, :], ramp[:], ACT.Exp, scale=z[:, n:n + 1]), a_k)
            if n in LN_STEPS:
                ln_ready[LN_STEPS[n]] = next(norms[LN_STEPS[n]])
            if n in scale_at:
                scale_weights(*scale_at[n])
            if n in FORWARD_AT:
                pe.wait(forward_here)
                forward_chunk(0, (FORWARD_ORDER[FORWARD_AT.index(n)],))
            if r in ON_VECTOR:
                c = on_vector % CHAINS
                dve.wait(decayed, chain_sum[c])
                if on_vector < CHAINS:
                    chain_sum[c] = dve.do(lambda e, n=n, r=r, c=c: e.tensor_scalar(
                        chain[:, c, :], decay[:, r, :], c_re[:, n:n + 1], None, ALU.mult), v_k)
                else:
                    chain_sum[c] = dve.do(lambda e, n=n, r=r, c=c: e.scalar_tensor_tensor(
                        out=chain[:, c, :], in0=decay[:, r, :], scalar=c_re[:, n:n + 1],
                        in1=chain[:, c, :], op0=ALU.mult, op1=ALU.add), v_k)
                slot_read[r] = chain_sum[c]
                on_vector += 1
            else:
                dve.wait(spread_read[r])
                diagonal = dve.do(lambda e, n=n, r=r: e.tensor_scalar(spread[:, r, :], eye[:], c_re[:, n:n + 1], None,
                                                                      ALU.mult), v_k)
                pe.wait(decayed, diagonal)
                slot_read[r] = spread_read[r] = add_taps(decay[:, r, :], spread[:, r, :])
        dve.wait(*chain_sum)
        skip_done = dve.do(lambda e: e.tensor_tensor(chain[:, 0, 0:1], chain[:, 0, 0:1], skip_d[:], ALU.add), v_k)
        pe.wait(skip_done)
        add_taps(chain[:, 1, :], eye[:])
        turned = add_taps(chain[:, 0, :], eye[:], final=True)
        act.wait(turned)
        for h, (bank, _, free) in enumerate(halves):
            ktap_done = act.do(lambda e, h=h, bank=bank: e.copy(ktap[:, h, :], bank[:, 0:P]), a_k)
            free.append(ktap_done)
        pe.wait(dft_here, ktap_done)
        for lo, hi in ((0, 4), (4, 5)):
            bank, before, free = misc.take()
            pe.wait(*before)
            for i in range(lo, hi):
                for h in range(HALVES):
                    done = pe.do(lambda e, i=i, h=h, lo=lo, bank=bank: e.matmul(
                        bank[:, (i - lo) * P:(i - lo + 1) * P], taps[:, h, i * P:(i + 1) * P], ktap[:, h, :],
                        start=(h == 0), stop=(h == HALVES - 1)), p_k if h == HALVES - 1 else None)
            act.wait(done)
            khat_done = act.do(lambda e, lo=lo, hi=hi, bank=bank: e.copy(khat[:, lo:hi, :], bank[:, 0:(hi - lo) * P]),
                               a_k)
            free.append(khat_done)

        cut_weights()
        ln_ready[1] = next(norms[1])
        next(norms[2])
        dve.wait(khat_done)
        for ch in range(CONV_CHUNKS):
            products(ch)
            weights_cut = low_weights(ch, CONV_CHUNKS)
            if ch + 2 < CONV_CHUNKS:
                ln_ready[ch + 2] = next(norms[ch + 2])
            if ch + 3 < CONV_CHUNKS:
                next(norms[ch + 3])
            if ch:
                residual(ch - 1)
            if ch == 2:
                pe.wait(expw_here)
                dve.wait(expw_here)
            if ch >= 2:
                next(first, None)
            if ch + 1 < CONV_CHUNKS:
                forward_chunk(ch + 1)
            if ch == 2:
                next(first)
            inverse_chunk(ch)
        residual(CONV_CHUNKS - 1)
        conv_ctx.close()
        conv_over = [conv_done[-1], inv_done[CONV_CHUNKS - 1, HALVES - 1][2], weights_cut]
        kept_x = nc.dram_tensor("kept_x", [P, TILES, D], F32, kind="Internal").ap()
        for ch in range(CONV_CHUNKS):
            tiles = slice(ch * tiles_per, (ch + 1) * tiles_per)
            sync.wait(conv_done[ch])
            kept = sync.dma(lambda e, tiles=tiles: e.dma_start(kept_x[:, tiles], stream[:, tiles]), s_kept)

        ROWS = 2 * LANES * HD
        scratch = nc.dram_tensor("qk_parts", [2, ROWS, QUADS, SETS + 1, SEQ], F16, kind="Internal").ap()
        att = ExitStack()

        def asb(name, shape, dt=F32):
            return att.enter_context(nc.sbuf_tensor(name, shape, dt))

        at_x = asb("at_x", [P, 2, 2, SEQ], F16)
        parts = asb("parts", [P, 2, 2, SETS + 1, SEQ], F16)
        qstack = asb("qstack", [P, 2, QUADS, SETS + 1, SEQ], F16)
        kfull = asb("kfull", [P, 2, QUADS, SEQ], F16)
        kstack = asb("kstack", [P, 2, LANES, QUADS, SEQ], F16)
        vstack = asb("vstack", [P, 2, HALVES, HEADS, SLOT])
        p_a, a_a, v_a, g_a = sig("tensor_attn"), sig("scalar_attn"), sig("vector_attn"), sig("gpsimd_attn")
        s_parts = [sig(f"landed_parts{i}") for i in range(2)]
        s_stack = [sig(f"landed_stack{i}") for i in range(2)]

        pool.wait(*conv_over)
        pool.wait(pool.do(lambda e: e.memset(vstack[:], 0.0), g_a))
        zeroed = pool.do(lambda e: e.memset(vstack[:, :, :, :, HD:HD + 1], 1.0), g_a)
        slot_free = {"x": [None] * 2, "parts": [None] * 2, "stack": [None] * 2, "kfull": [None] * 2, "v": [None] * 2,
                     "scratch": [None] * 2}
        ready = {}

        def attn_prologue(b):
            s = b % 2
            normed_done = mixed_normed[HALVES * b // FFN_TILES]
            bank, before, free = misc.take()
            pe.wait(normed_done, *before)
            for h in range(HALVES):
                done = pe.do(lambda e, h=h, bank=bank: e.transpose(bank[:, h * P:(h + 1) * P],
                                                                   normed[:, HALVES * b + h, :], eye[:]),
                             p_a if h == HALVES - 1 else None)
            act.wait(done, slot_free["x"][s])
            x_high = act.do(lambda e, bank=bank: e.copy(at_x[:, s, 0, :], bank[:, 0:SEQ]), a_a)
            dve.wait(x_high)
            x_done = dve.do(lambda e, bank=bank: e.tensor_tensor(at_x[:, s, 1, :], bank[:, 0:SEQ], at_x[:, s, 0, :],
                                                                 ALU.subtract), v_a)
            free.append(x_done)
            yield
            for g0 in range(0, SETS + 1, 2):
                n = min(2, SETS + 1 - g0)
                bank, before, free = misc.take()
                pe.wait(x_done, *before)
                for g in range(g0, g0 + n):
                    for w_part, x_part in PRODUCTS:
                        done = pe.do(lambda e, g=g, w_part=w_part, x_part=x_part, g0=g0, bank=bank: e.matmul(
                            bank[:, (g - g0) * SEQ:(g - g0 + 1) * SEQ], wqkv_parts[:, w_part, g, :],
                            at_x[:, s, x_part, :], start=((w_part, x_part) == PRODUCTS[0]),
                            stop=((w_part, x_part) == PRODUCTS[-1])),
                            p_a if g == g0 + n - 1 and (w_part, x_part) == PRODUCTS[-1] else None)
                act.wait(done, slot_free["parts"][s])
                src = bank[:, 0:n * SEQ].rearrange("p (g t) -> p g t", t=SEQ)
                hi = act.do(lambda e, g0=g0, n=n, src=src: e.mul(parts[:, s, 0, g0:g0 + n, :], src, 1.0 / WSCALE), a_a)
                dve.wait(hi)
                lo = dve.do(lambda e, g0=g0, n=n, src=src: e.scalar_tensor_tensor(
                    out=parts[:, s, 1, g0:g0 + n, :], in0=src, scalar=1.0 / WSCALE,
                    in1=parts[:, s, 0, g0:g0 + n, :], op0=ALU.mult, op1=ALU.subtract), v_a)
                free.append(lo)
                yield
            sync.wait(lo, hi, slot_free["scratch"][s])
            for c in range(QUADS):
                wrote = sync.dma(lambda e, c=c: e.dma_start(
                    scratch[s].rearrange("(a r) c g t -> r a c (g t)", a=2)[:, :, c],
                    parts[c * SLOT:(c + 1) * SLOT, s].rearrange("r a g t -> r a (g t)")), s_parts[s])
            slot_free["parts"][s] = wrote
            sync.wait(wrote, slot_free["stack"][s], slot_free["kfull"][s])
            twice = scratch[s:s + 1].rearrange("a r c g t -> a r (c g t)").to_broadcast([2, ROWS, QUADS * (SETS + 1) * SEQ])
            sync.dma(lambda e: e.dma_start(qstack[:, s].rearrange("p c g t -> p (c g t)"), twice), s_stack[s])
            krows = scratch[s][:, :, SETS, :]
            half = ROWS // 2
            sync.dma(lambda e: e.dma_start(kfull[0:ROWS, s], krows), s_stack[s])
            sync.dma(lambda e: e.dma_start(kfull[ROWS:ROWS + half, s], krows[half:ROWS]), s_stack[s])
            stacked = sync.dma(lambda e: e.dma_start(kfull[ROWS + half:P, s], krows[0:half]), s_stack[s])
            slot_free["scratch"][s] = stacked
            yield
            bank, before, free = misc.take()
            pe.wait(*before)
            for h in range(HALVES):
                for w_part, x_part in PRODUCTS:
                    done = pe.do(lambda e, h=h, w_part=w_part, x_part=x_part, bank=bank: e.matmul(
                        bank[:, h * P:(h + 1) * P], at_x[:, s, x_part, h * P:(h + 1) * P],
                        wqkv_parts[:, w_part, SETS + 1, :],
                        start=((w_part, x_part) == PRODUCTS[0]), stop=((w_part, x_part) == PRODUCTS[-1])),
                        p_a if h == HALVES - 1 and (w_part, x_part) == PRODUCTS[-1] else None)
            slot_free["x"][s] = done
            act.wait(done, zeroed, slot_free["v"][s])
            v_done = act.do(lambda e, bank=bank: e.mul(
                vstack[:, s, :, :, 0:HD].rearrange("p h n d -> p (h n) d"),
                bank[:, 0:HALVES * D].rearrange("p (n d) -> p n d", d=HD), 1.0 / WSCALE), a_a)
            free.append(v_done)
            for _ in range(7):
                yield
            dve.wait(stacked, slot_free["stack"][s])
            for lane in range(LANES):
                spread = dve.do(lambda e, lane=lane: e.tensor_scalar(
                    kstack[:, s, lane].rearrange("p c t -> p (c t)"), kfull[:, s].rearrange("p c t -> p (c t)"),
                    lanes[:, lane:lane + 1], None, ALU.mult), v_a)
            slot_free["kfull"][s] = spread
            ready[b] = (spread, v_done, stacked)

        attn_first = attn_prologue(0)
        pe.wait(weights_cut)
        dve.wait(weights_cut)
        for q_ in (pe, act, dve):
            q_.wait(attw_here)
        experts_over = run_first(first, conv_over)

        prob = asb("prob", [P, 3, LANES, UNIT])
        o_tok = asb("o_tok", [P, 2, BANK])
        o_norm = asb("o_norm", [P, 2, PAIRS, 2 * 2 * LANES, SLOT])
        rden = asb("rden", [P, 2, QUADS * PAIRS, 2 * 2 * LANES])
        in_range = asb("in_range", [P, QUADS * PAIRS * 2 * 2 * LANES])
        o_rows = asb("o_rows", [P, PAIRS, HALVES, 2, P])
        for q_ in (pe, act, dve, pool):
            q_.wait(experts_over)
        score_banks = [psum[:, 2 * i * BANK:2 * i * BANK + UNIT] for i in range(2)]
        score_free = [wide.free[2 * i] + wide.free[2 * i + 1] for i in range(2)]
        units = [0]
        SHARES = ((320, 2 * SEQ), (160, 320), (0, 160))
        POOL_LANES = (0, 1)
        probs_free = [None] * 3

        def scores(b, grp, lane):
            c, pair = divmod(grp, PAIRS)
            s, u, pb = b % 2, units[0] % 2, (b * QUADS * PAIRS + grp) % 3
            units[0] += 1
            qs = qstack[:, s, c, 2 * pair:2 * pair + 2, :]
            sbk = score_banks[u]
            pe.wait(ready[b][0], ready[b][2], *score_free[u])
            pe.do(lambda e: e.matmul(sbk[:, 0:2 * SEQ], kstack[:, s, lane, c, 0:P],
                                     qs.rearrange("p g (h q) -> p h g q", q=P), start=True, stop=True))
            done = pe.do(lambda e: e.matmul(sbk[:, 2 * SEQ:UNIT], kstack[:, s, lane, c, P:SEQ],
                                            qs[:, :, P:SEQ], start=True, stop=True), p_a)
            if grp == QUADS * PAIRS - 1 and lane == LANES - 1:
                slot_free["stack"][s] = done
            act.wait(done, probs_free[pb])
            ex = act.do(lambda e: e.activation(prob[:, pb, lane, :], sbk, ACT.Exp, scale=SCALE), a_a)
            score_free[u] = [ex]
            eng, sg = (pool, g_a) if lane in POOL_LANES else (dve, v_a)
            diag = prob[:, pb, lane, :].rearrange("p (n q) -> p n q", q=2 * P)[:, 0:3:2, :]
            eng.wait(ex)
            return eng.do(lambda e: e.tensor_tensor(
                diag, diag, keep[:].rearrange("p (a q) -> p a q", a=1).to_broadcast([P, 2, 2 * P]), ALU.mult), sg), ex

        def weighted(b, grp, part, masked, bank, before=()):
            c, _ = divmod(grp, PAIRS)
            s, pb = b % 2, (b * QUADS * PAIRS + grp) % 3
            pe.wait(*before, ready[b][1])
            last_part = part == len(SHARES)
            cols = slice(SEQ, 2 * SEQ) if last_part else slice(*SHARES[part])
            keys, ins = (1, slice(2 * SEQ, UNIT)) if last_part else (0, cols)
            unmasked = not last_part and cols.start >= SEQ
            for mask_done, ex in masked:
                pe.wait(ex if unmasked else mask_done)
            for lane in range(LANES):
                done = pe.do(lambda e, lane=lane: e.matmul(
                    bank[SLOT * lane:SLOT * (lane + 1), cols], vstack[:, s, keys, c * LANES + lane, :],
                    prob[:, pb, lane, ins], start=(part == 0), stop=last_part),
                    p_a if last_part and lane == LANES - 1 else None)
            if last_part:
                probs_free[pb] = done
                if grp == QUADS * PAIRS - 1:
                    slot_free["v"][s] = done
            return done

        def turn(b, grp, bank, free, done):
            s, r = b % 2, grp % 2
            c, pair = divmod(grp, PAIRS)
            dve.wait(done)
            turned = dve.do(lambda e: e.transpose(o_tok[:, r, :], bank), v_a)
            free.append(turned)
            heads = o_tok[:, r, :].rearrange("p (n r) -> p n r", r=SLOT)
            rd = rden[:, s, grp, :].rearrange("p (n a) -> p n a", a=1)
            dve.wait(turned)
            rec = dve.do(lambda e: e.reciprocal(rd, heads[:, :, HD:HD + 1]), v_a)
            dve.wait(rec)
            return dve.do(lambda e: e.tensor_tensor(
                o_norm[:, s, pair, :, c * HD:(c + 1) * HD], heads[:, :, 0:HD],
                rd.to_broadcast([P, 2 * 2 * LANES, HD]), ALU.mult), v_a)

        attn_done = {}
        rows_free = [None]
        counted = [None]

        def attn_epilogue(b, nrm):
            s = b % 2
            dve.wait(nrm, rows_free[0])
            rows_done = dve.do(lambda e: e.transpose(o_rows[:].rearrange("p a h k t -> p (a h k t)"),
                                                     o_norm[:, s].rearrange("p a n r -> p (a n r)")), v_a)
            rd = rden[:, s].rearrange("p g n -> p (g n)")
            low = dve.do(lambda e: e.tensor_scalar(in_range[:], rd, RDEN_MIN, None, ALU.is_ge), v_a)
            dve.wait(low)
            counted[0] = dve.do(lambda e: e.scalar_tensor_tensor(
                out=in_range[:], in0=rd, scalar=RDEN_MAX, in1=in_range[:], op0=ALU.is_le, op1=ALU.mult,
                accum_out=good[:, b:b + 1]), v_a)
            yield
            bank, before, free = misc.take()
            pe.wait(rows_done, *before)
            for h in range(HALVES):
                for g in range(SETS):
                    final = g == SETS - 1 and h == HALVES - 1
                    done = pe.do(lambda e, g=g, h=h, bank=bank: e.matmul(
                        bank[:, h * P:(h + 1) * P], o_rows[:, g // 2, h, g % 2, :], wproj[:, g, :], start=(g == 0),
                        stop=(g == SETS - 1)), p_a if final else None)
            rows_free[0] = done
            dve.wait(done, kept)
            tiles = slice(HALVES * b, HALVES * (b + 1))
            added = dve.do(lambda e: e.tensor_tensor(stream[:, tiles, :], bank[:, 0:SEQ].rearrange(
                "p (h m) -> p h m", h=HALVES), mixed[:, tiles, :], ALU.add), v_a)
            free.append(added)
            attn_done[b] = added
            yield

        for _ in attn_first:
            pass

        def store(ch, acc, crew):
            crew.sync.wait(acc)
            t0 = ch * FFN_TILES
            crew.sync.dma(lambda e: e.dma_start(out_tiles[:, t0:t0 + FFN_TILES, :], mixed[:, t0:t0 + FFN_TILES, :]),
                          crew.stored)

        def judge():
            dve.wait(counted[0])
            counted[0] = dve.do(lambda e: e.reduce_sum(good[:, BATCH:BATCH + 1], good[:, 0:BATCH], AX_X), v_a)
            bank, before, free = misc.take()
            pe.wait(counted[0], *before)
            turned = pe.do(lambda e: e.transpose(bank[0:1, 0:P], good[:, BATCH:BATCH + 1], eye[:]), p_a)
            dve.wait(turned)
            counted[0] = dve.do(lambda e: e.reduce_sum(good[0:1, 0:1], bank[0:1, 0:P], AX_X), v_a)
            free.append(counted[0])
            yield
            dve.wait(counted[0])
            judged = dve.do(lambda e: e.tensor_scalar(bad_scores[:], good[0:1, 0:1],
                                                      float(BATCH * SEQ * HEADS * SETS) - 0.5, None, ALU.is_lt), v_a)
            dve.wait(judged)
            dve.do(lambda e: e.tensor_tensor(bad[:], bad_scores[:], bad_weights[:], ALU.max), v_a)
            yield

        judging = judge()

        def tick_second(ch, e_):
            if (ch, e_) >= (0, 2):
                next(judging, None)

        second, run_second = moe("second", main_crew, False, rings, front, stream, mixed,
                                 lambda t: attn_done[t // HALVES], lambda ch, acc: store(ch, acc, main_crew),
                                 tick_second)
        NG = QUADS * PAIRS
        steps = [(b, g) for b in range(BATCH) for g in range(NG)]
        ahead, behind = iter(()), iter(())
        masked, open_sum = {}, None
        for n in range(len(steps) + 2):
            now = steps[n] if n < len(steps) else None
            back = steps[n - 1] if 1 <= n <= len(steps) else None
            if now and now[1] == 0:
                for _ in ahead:
                    pass
                ahead = attn_prologue(now[0] + 1) if now[0] + 1 < BATCH else spaced(second)
                if now[0] in (1, 2):
                    next(norm_steps[FFN_CHUNKS - 1])
            if now:
                masked[now] = [scores(*now, 0)]
            if open_sum:
                older, bank, before, free = open_sum
                done = weighted(*older, len(SHARES), masked.pop(older), bank)
                nrm = turn(*older, bank, free, done)
                if older[1] == NG - 1:
                    for _ in behind:
                        pass
                    behind = attn_epilogue(older[0], nrm)
                open_sum = None
            next(ahead, None)
            if now:
                masked[now].append(scores(*now, 1))
            if back:
                open_sum = (back, *narrow.take())
                weighted(*back, 0, masked[back], *open_sum[1:3])
            if now:
                masked[now].append(scores(*now, 2))
            if back:
                weighted(*back, 1, masked[back], open_sum[1])
            next(ahead, None)
            if now:
                masked[now].append(scores(*now, 3))
            if back:
                weighted(*back, 2, masked[back], open_sum[1])
            next(behind, None)
        for _ in behind:
            pass
        att.close()
        for pair in range(2):
            for bank_free in wide.free[2 * pair:2 * pair + 2]:
                bank_free[:] = score_free[pair]

        run_second(second, [(sg, sg.value) for sg in (p_a, a_a, v_a, g_a)])
        sync.wait((main_crew.stored, main_crew.stored.value))

        main_over = main_crew.issued() + [(v_a, v_a.value)]

        def general_rings():
            return Banks(psum, [6, 7]), Banks(psum, [0, 1, 2, 3]), Banks(psum, [4, 5])

        def run_whole(tag, start, after_chunk):
            crew = Crew(ctx, nc, tag)
            for q_ in crew.streams:
                q_.wait(*start)
            if tag == "general_first":
                crew.dve.wait(crew.sync.dma(lambda e: e.dma_start(stream[:], kept_x), crew.stored))
            prologue, run = moe(tag, crew, True, general_rings(), front, stream, mixed, lambda t: None,
                                lambda ch, acc: after_chunk(ch, acc, crew), lambda ch, e_: None)
            run(prologue, [])
            for q_ in crew.streams:
                q_.wait(*crew.issued())
            return crew

        def norm_at_once(ch, acc, crew):
            for _ in norm_mixed(ch, acc, crew, {}):
                pass

        general_first = run_whole("general_first", main_over, norm_at_once)
        attention = general_attention(ctx, nc, dr, psum, general_first.issued(), mixed, normed, stream, wqkv, wproj, eye)
        general_second = run_whole("general_second", [], store)
        for q_, before, during, after in zip(main_crew.streams, general_first.streams, attention,
                                             general_second.streams):
            def whole_path(e, before=before, during=during, after=after):
                before.play(e)
                during(e)
                after.play(e)
            q_.wait(*main_over)
            q_.branch(bad, whole_path)

        block = ctx.enter_context(nc.Block())
        block.sync(lambda e: sync.play(e))
        block.gpsimd(lambda e: pool.play(e))
        block.scalar(lambda e: act.play(e))
        block.vector(lambda e: dve.play(e))
        block.tensor(lambda e: pe.play(e))


OUT_SHAPE = (BATCH, SEQ, D)


def kernel(**inputs):
    import concourse.bacc as bacc
    from concourse.bass_utils import run_bass_kernel_spmd

    arrays = {k: np.ascontiguousarray(v) for k, v in inputs.items()
              if k not in ("L0_attn_b_W_attn", "L0_attn_b_W_proj", "L0_ffn_b1", "L0_attn_a_C_im")}
    arrays["w_attn_cols"] = np.ascontiguousarray(np.asarray(inputs["L0_attn_b_W_attn"]).T)
    arrays["w_proj_rows"] = np.ascontiguousarray(
        np.asarray(inputs["L0_attn_b_W_proj"]).T.reshape(SETS, QUADS, LANES, HD, D).transpose(2, 1, 3, 0, 4)
        .reshape(P, SETS, D))
    arrays["b1_cols"] = np.ascontiguousarray(np.asarray(inputs["L0_ffn_b1"]).reshape(EXPERTS * HBLK, P).T)
    arrays.update(shape_constants())
    nc = bacc.Bacc("TRN2", target_bir_lowering=False, num_devices=1)
    dr = {k: nc.dram_tensor(k, a.shape, mybir.dt.from_np(a.dtype), kind="ExternalInput").ap()
          for k, a in arrays.items()}
    out = nc.dram_tensor("out", OUT_SHAPE, F32, kind="ExternalOutput").ap()
    build(nc, dr, out)
    r = run_bass_kernel_spmd(nc, [arrays], core_ids=[0])
    return r.results[0]["out"]
```
